# Optimizing a Trainium2 kernel written in Bass

```python
import numpy as np
import jax
import jax.numpy as jnp

def _softmax(x, axis=-1):
    return jax.nn.softmax(x, axis=axis)

def _gelu(x):
    return jax.nn.gelu(x, approximate=True)

def _silu(x):
    return jax.nn.silu(x)

def _sigmoid(x):
    return jax.nn.sigmoid(x)

def _layernorm(x, axis=-1, eps=1e-05):
    m = jnp.mean(x, axis=axis, keepdims=True)
    v = jnp.var(x, axis=axis, keepdims=True)
    return (x - m) / jnp.sqrt(v + eps)

def _scatter_add(tgt, idx, src, axis=0):
    return tgt.at[idx].add(src)

def _segment_sum(src, seg, n):
    return jax.ops.segment_sum(src, seg, n)
kernel_name = 'mk_vit_tower_d1_tok_img768_r4_b8002a'

def setup_inputs(seed: int=0):
    np.random.seed(seed)
    _w = jnp.asarray

    def _rec_inputs():
        import jax
        import jax.numpy as jnp
        _rk = jax.random.key(seed)
        x = -0.00016672 + 0.999947 * jax.random.normal(jax.random.fold_in(_rk, 1), (32, 3, 96, 96), jnp.float32)
        return x
    x = _rec_inputs()

    def _L0_tok_setup():
        import jax, jax.numpy as jnp
        import numpy as np
        B, C, H, Wd = (64, 3, 96, 96)
        PH = PW = 16
        NH, NW = (H // PH, Wd // PW)
        NP = NH * NW
        PD = C * PH * PW
        ED = 192
        EPS = 1e-05

        def layernorm(x, g, b):
            mu = jnp.mean(x, axis=-1, keepdims=True)
            var = jnp.mean(jnp.square(x - mu), axis=-1, keepdims=True)
            return (x - mu) * jax.lax.rsqrt(var + EPS) * g + b
        key = jax.random.key(seed)
        ks = jax.random.split(key, 6)
        return {'x': jax.random.normal(ks[0], (B, C, H, Wd), dtype=jnp.float32), 'ln1_g': jnp.ones((PD,), jnp.float32), 'ln1_b': jnp.zeros((PD,), jnp.float32), 'W': jax.random.normal(ks[1], (PD, ED), dtype=jnp.float32) * 0.02, 'b': jnp.zeros((ED,), jnp.float32), 'ln2_g': jnp.ones((ED,), jnp.float32), 'ln2_b': jnp.zeros((ED,), jnp.float32), 'cls_token': jax.random.normal(ks[2], (ED,), dtype=jnp.float32), 'pos_embed': jax.random.normal(ks[3], (1, NP + 1, ED), dtype=jnp.float32) * 0.02}
    _L0_tok_all = _L0_tok_setup()
    _L0_tok_in = {k: v for k, v in _L0_tok_all.items() if k in ('ln1_g', 'ln1_b', 'W', 'b', 'ln2_g', 'ln2_b', 'cls_token', 'pos_embed')}
    del _L0_tok_all

    def _L0_attn_setup():
        import jax, jax.numpy as jnp
        import numpy as np
        D = 192
        ORDER = 2
        K = 3
        MAXLEN = 512

        def _fft_conv(h, x, Bp):
            L = x.shape[-1]
            n = 2 * L
            h_f = jnp.fft.rfft(h, n=n, norm='forward')
            x_f = jnp.fft.rfft(x, n=n)
            y = jnp.fft.irfft(h_f * x_f, n=n, norm='forward')[..., :L]
            return y + x * Bp
        key = jax.random.key(seed)
        ks = jax.random.split(key, 8)
        Bsz, L = (4, 512)
        C = D * (ORDER + 1)
        u = jax.random.normal(ks[0], (Bsz, L, D), jnp.float32)
        W_lin = jax.random.normal(ks[1], (C, D), jnp.float32) / np.float32(np.sqrt(D))
        b_lin = jnp.zeros((C,), jnp.float32)
        conv_w = jax.random.normal(ks[2], (C, 1, K), jnp.float32) / np.float32(np.sqrt(K))
        conv_b = jnp.zeros((C,), jnp.float32)
        W_out = jax.random.normal(ks[3], (D, D), jnp.float32) / np.float32(np.sqrt(D))
        b_out = jnp.zeros((D,), jnp.float32)
        h_param = jax.random.normal(ks[4], (ORDER, D, MAXLEN), jnp.float32)
        win_b = jnp.zeros((1, D, 1), jnp.float32)
        min_decay = np.log(0.01) / 1.5
        max_decay = np.log(0.01) / 0.3
        alphas = jnp.linspace(min_decay, max_decay, D, dtype=jnp.float32)[None, :, None]
        Bmat = jax.random.normal(ks[5], (ORDER, 1, D, 1), jnp.float32)
        return dict(u=u, W_lin=W_lin, b_lin=b_lin, conv_w=conv_w, conv_b=conv_b, W_out=W_out, b_out=b_out, h_param=h_param, win_b=win_b, alphas=alphas, Bmat=Bmat)
    _L0_attn_all = _L0_attn_setup()
    _L0_attn_in = {k: v for k, v in _L0_attn_all.items() if k in ('W_lin', 'b_lin', 'conv_w', 'conv_b', 'W_out', 'b_out', 'h_param', 'win_b', 'alphas', 'Bmat')}
    del _L0_attn_all

    def _L0_ffn_setup():
        import jax, jax.numpy as jnp
        import numpy as np
        D = 192
        I = 768
        E = 8
        K = 2
        LIMIT = 10.0
        VOCAB = 8192

        def _expert(xf, W1, W2, W3):
            gate = jnp.minimum(xf @ W1, LIMIT)
            up = jnp.clip(xf @ W3, -LIMIT, LIMIT)
            return jax.nn.silu(gate) * up @ W2
        key = jax.random.key(seed)
        ks = jax.random.split(key, 10)
        s = 0.02
        return {'x': jax.random.normal(ks[0], (1, 512, D), dtype=jnp.float32), 'input_ids': jax.random.randint(ks[1], (1, 512), 0, VOCAB, dtype=jnp.int64), 'gate_w': jax.random.normal(ks[2], (D, E), dtype=jnp.float32) * s, 'gate_bias': jnp.zeros((E,), dtype=jnp.float32), 'w1': jax.random.normal(ks[3], (E, D, I), dtype=jnp.float32) * s, 'w2': jax.random.normal(ks[4], (E, I, D), dtype=jnp.float32) * s, 'w3': jax.random.normal(ks[5], (E, D, I), dtype=jnp.float32) * s, 'w1s': jax.random.normal(ks[6], (D, I), dtype=jnp.float32) * s, 'w2s': jax.random.normal(ks[7], (I, D), dtype=jnp.float32) * s, 'w3s': jax.random.normal(ks[8], (D, I), dtype=jnp.float32) * s}
    _L0_ffn_all = _L0_ffn_setup()
    _L0_ffn_in = {k: v for k, v in _L0_ffn_all.items() if k in ('input_ids', 'gate_w', 'gate_bias', 'w1', 'w2', 'w3', 'w1s', 'w2s', 'w3s')}
    del _L0_ffn_all
    return {'x': x, 'L0_tok_ln1_g': _L0_tok_in['ln1_g'], 'L0_tok_ln1_b': _L0_tok_in['ln1_b'], 'L0_tok_W': _L0_tok_in['W'], 'L0_tok_b': _L0_tok_in['b'], 'L0_tok_ln2_g': _L0_tok_in['ln2_g'], 'L0_tok_ln2_b': _L0_tok_in['ln2_b'], 'L0_tok_cls_token': _L0_tok_in['cls_token'], 'L0_tok_pos_embed': _L0_tok_in['pos_embed'], 'L0_attn_W_lin': _L0_attn_in['W_lin'], 'L0_attn_b_lin': _L0_attn_in['b_lin'], 'L0_attn_conv_w': _L0_attn_in['conv_w'], 'L0_attn_conv_b': _L0_attn_in['conv_b'], 'L0_attn_W_out': _L0_attn_in['W_out'], 'L0_attn_b_out': _L0_attn_in['b_out'], 'L0_attn_h_param': _L0_attn_in['h_param'], 'L0_attn_win_b': _L0_attn_in['win_b'], 'L0_attn_alphas': _L0_attn_in['alphas'], 'L0_attn_Bmat': _L0_attn_in['Bmat'], 'L0_ffn_input_ids': _L0_ffn_in['input_ids'], 'L0_ffn_gate_w': _L0_ffn_in['gate_w'], 'L0_ffn_gate_bias': _L0_ffn_in['gate_bias'], 'L0_ffn_w1': _L0_ffn_in['w1'], 'L0_ffn_w2': _L0_ffn_in['w2'], 'L0_ffn_w3': _L0_ffn_in['w3'], 'L0_ffn_w1s': _L0_ffn_in['w1s'], 'L0_ffn_w2s': _L0_ffn_in['w2s'], 'L0_ffn_w3s': _L0_ffn_in['w3s']}

def reference(x, L0_tok_ln1_g, L0_tok_ln1_b, L0_tok_W, L0_tok_b, L0_tok_ln2_g, L0_tok_ln2_b, L0_tok_cls_token, L0_tok_pos_embed, L0_attn_W_lin, L0_attn_b_lin, L0_attn_conv_w, L0_attn_conv_b, L0_attn_W_out, L0_attn_b_out, L0_attn_h_param, L0_attn_win_b, L0_attn_alphas, L0_attn_Bmat, L0_ffn_input_ids, L0_ffn_gate_w, L0_ffn_gate_bias, L0_ffn_w1, L0_ffn_w2, L0_ffn_w3, L0_ffn_w1s, L0_ffn_w2s, L0_ffn_w3s):
    import jax
    import jax.numpy as jnp

    def _L0_tok_ref(x, ln1_g, ln1_b, W, b, ln2_g, ln2_b, cls_token, pos_embed):
        import jax, jax.numpy as jnp
        import numpy as np
        B, C, H, Wd = (64, 3, 96, 96)
        PH = PW = 16
        NH, NW = (H // PH, Wd // PW)
        NP = NH * NW
        PD = C * PH * PW
        ED = 192
        EPS = 1e-05

        def layernorm(x, g, b):
            mu = jnp.mean(x, axis=-1, keepdims=True)
            var = jnp.mean(jnp.square(x - mu), axis=-1, keepdims=True)
            return (x - mu) * jax.lax.rsqrt(var + EPS) * g + b
        bsz = x.shape[0]
        p = x.reshape(bsz, C, NH, PH, NW, PW)
        p = p.transpose(0, 2, 4, 3, 5, 1).reshape(bsz, NP, PD)
        out = layernorm(p, ln1_g, ln1_b)
        out = jnp.einsum('bnp,pe->bne', out, W) + b
        out = layernorm(out, ln2_g, ln2_b)
        cls = jnp.broadcast_to(cls_token, (bsz, 1, ED))
        out = jnp.concatenate([cls, out], axis=1)
        out = out + pos_embed
        return out

    def _L0_attn_ref(u, W_lin, b_lin, conv_w, conv_b, W_out, b_out, h_param, win_b, alphas, Bmat):
        import jax, jax.numpy as jnp
        import numpy as np
        D = 192
        ORDER = 2
        K = 3
        MAXLEN = 512

        def _fft_conv(h, x, Bp):
            L = x.shape[-1]
            n = 2 * L
            h_f = jnp.fft.rfft(h, n=n, norm='forward')
            x_f = jnp.fft.rfft(x, n=n)
            y = jnp.fft.irfft(h_f * x_f, n=n, norm='forward')[..., :L]
            return y + x * Bp
        Bsz, L, d = u.shape
        z = (u @ W_lin.T + b_lin).transpose(0, 2, 1)
        z = jax.lax.conv_general_dilated(z, conv_w, window_strides=(1,), padding=[(K - 1, K - 1)], feature_group_count=z.shape[1], dimension_numbers=('NCH', 'OIH', 'NCH'))[..., :L] + conv_b[None, :, None]
        xs = [z[:, i * d:(i + 1) * d] for i in range(ORDER)]
        v = z[:, ORDER * d:] + u.transpose(0, 2, 1)
        t = jnp.linspace(0.0, 1.0, MAXLEN, dtype=u.dtype)[None, None, :L]
        h = h_param[:, :, :L] * (jnp.exp(alphas * t) + win_b)
        h = h / jnp.sum(jnp.abs(h), axis=-2, keepdims=True)
        for i in range(ORDER):
            v = v + jax.nn.softmax(xs[i], axis=1) * _fft_conv(h[i][None], v, Bmat[i])
        v = v.transpose(0, 2, 1)
        return v + v @ W_out.T + b_out

    def _L0_ffn_ref(x, input_ids, gate_w, gate_bias, w1, w2, w3, w1s, w2s, w3s):
        import jax, jax.numpy as jnp
        import numpy as np
        D = 192
        I = 768
        E = 8
        K = 2
        LIMIT = 10.0
        VOCAB = 8192

        def _expert(xf, W1, W2, W3):
            gate = jnp.minimum(xf @ W1, LIMIT)
            up = jnp.clip(xf @ W3, -LIMIT, LIMIT)
            return jax.nn.silu(gate) * up @ W2
        B, T, _ = x.shape
        flat = x.reshape(-1, D)
        N = flat.shape[0]
        scores = jnp.sqrt(jax.nn.softplus(flat @ gate_w))
        routed_scores = scores + gate_bias
        _, indices = jax.lax.top_k(routed_scores, K)
        weights = jnp.take_along_axis(scores, indices, axis=1)
        weights = weights / jnp.clip(weights.sum(axis=-1, keepdims=True), 1e-06)
        combine = jnp.zeros((N, E), dtype=weights.dtype)
        combine = combine.at[jnp.arange(N)[:, None], indices].add(weights)
        y = _expert(flat, w1s, w2s, w3s)
        gate_h = jnp.minimum(jnp.einsum('td,edi->eti', flat, w1), LIMIT)
        up_h = jnp.clip(jnp.einsum('td,edi->eti', flat, w3), -LIMIT, LIMIT)
        h = jax.nn.silu(gate_h) * up_h
        out_e = jnp.einsum('eti,eid->etd', h, w2)
        routed = jnp.einsum('etd,te->td', out_e, combine)
        return (y + routed).reshape(B, T, D)
    h = _L0_tok_ref(x, L0_tok_ln1_g, L0_tok_ln1_b, L0_tok_W, L0_tok_b, L0_tok_ln2_g, L0_tok_ln2_b, L0_tok_cls_token, L0_tok_pos_embed)
    h = h + _L0_attn_ref(_layernorm(h, axis=-1), L0_attn_W_lin, L0_attn_b_lin, L0_attn_conv_w, L0_attn_conv_b, L0_attn_W_out, L0_attn_b_out, L0_attn_h_param, L0_attn_win_b, L0_attn_alphas, L0_attn_Bmat)
    h = h + _L0_ffn_ref(_layernorm(h, axis=-1), L0_ffn_input_ids, L0_ffn_gate_w, L0_ffn_gate_bias, L0_ffn_w1, L0_ffn_w2, L0_ffn_w3, L0_ffn_w1s, L0_ffn_w2s, L0_ffn_w3s)
    return h

_drawn_inputs = setup_inputs


def setup_inputs(seed=0):
    import zlib

    import numpy as np

    out = dict(_drawn_inputs(seed))
    spreads = {'L0_tok_ln1_g': (1.0, 0.2),
     'L0_tok_ln1_b': (0.0, 0.1),
     'L0_tok_b': (0.0, 0.1),
     'L0_tok_ln2_g': (1.0, 0.2),
     'L0_tok_ln2_b': (0.0, 0.1),
     'L0_attn_b_lin': (0.0, 0.1),
     'L0_attn_conv_b': (0.0, 0.1),
     'L0_attn_b_out': (0.0, 0.1),
     'L0_attn_win_b': (0.0, 0.8),
     'L0_ffn_gate_bias': (0.0, 0.8)}
    factors = {'L0_tok_pos_embed': 2.95,
     'L0_attn_h_param': 8.0,
     'L0_attn_alphas': 8.0,
     'L0_ffn_gate_w': 8.0,
     'L0_ffn_w1': 8.0,
     'L0_ffn_w2': 8.0,
     'L0_ffn_w3': 8.0,
     'L0_ffn_w1s': 7.273,
     'L0_ffn_w2s': 7.224,
     'L0_ffn_w3s': 7.214}
    for name, (base, spread) in spreads.items():
        noise = np.random.default_rng([zlib.crc32(name.encode()), seed]).standard_normal(out[name].shape)
        drawn = base * np.exp(spread * noise) if base else spread * noise
        out[name] = jnp.asarray(drawn.astype(out[name].dtype))
    for name, factor in factors.items():
        out[name] = (out[name] * factor).astype(out[name].dtype)
    return out
```

```python
from contextlib import ExitStack

import concourse.bass as bass
from concourse import mybir

ALU = mybir.AluOpType
ACT = mybir.ActivationFunctionType
F32 = mybir.dt.float32
AX = mybir.AxisListType

P = 128
B = 32
HB = 2
BH = B // HB
L = 37
LT = P // BH
TH = -(-L // LT)
LP = TH * LT
TILES = HB * TH
COLS = LP * BH
REAL = L * BH
PD = 768
FC = PD // P
D = 192
DT = D - P
ORDER = 2
E = 8
I = 768
IC = I // P
EPS = 1e-5
LIMIT = 10.0
SILU_LIMIT = 9.999546021312975
SPLIT = COLS // 2
NX = E + 1
C_BLIN, C_TAP, C_CONVB, C_ALPHA, C_WINB, C_BMAT = 0, 3, 12, 15, 16, 17
NCH = C_BMAT + ORDER


def build(nc, xtok, xfeat, pos, ident, steps, w_in, g1, b1, rows, cls, wlin_m, wlin_t, chan_m, chan_t,
          hp_m, hp_t, wout_m, wout_t, gate_m, gate_t, gate_b, w1, w3, w2, out):
    with ExitStack() as ctx:
        def sb(name, shape, dt=F32):
            return ctx.enter_context(nc.sbuf_tensor(name, shape, dt))

        def sem(name):
            return ctx.enter_context(nc.semaphore(name))

        ps = ctx.enter_context(nc.psum_tensor("ps", [P, 8, 512], F32))
        ps_tok = ps[:, 0:6, :].rearrange("p (a b) (h n) -> p a (b h) n", a=HB, h=2)
        ps_flat = ps[:, :, :].rearrange("p b n -> p (b n)")

        id_sb = sb("id_sb", [P, P])
        ones = sb("ones", [P, P])
        w_sb = sb("w_sb", [P, FC, D])
        wg_sb = sb("wg_sb", [P, FC, D])
        g1_sb = sb("g1_sb", [P, FC])
        b1_sb = sb("b1_sb", [P, FC])
        b1_wide = sb("b1_wide", [P, FC, P])
        rows_sb = sb("rows_sb", [P, 4, D])
        pos_sb = sb("pos_sb", [P, TH, D])
        cls_sb = sb("cls_sb", [BH, D])
        colsum = sb("colsum", [P, D])
        shift = sb("shift", [P, D])
        wlin = [sb("wlin_m_sb", [P, 3 * D]), sb("wlin_t_sb", [P, 3 * D])]
        chan = [sb("chan_m_sb", [P, NCH]), sb("chan_t_sb", [P, NCH])]
        hp = [sb("hp_m_sb", [P, ORDER, L]), sb("hp_t_sb", [P, ORDER, L])]
        habs = [sb("habs_m", [P, ORDER, L]), sb("habs_t", [P, ORDER, L])]
        win = [sb("win_m", [P, L]), sb("win_t", [P, L])]
        hrec = sb("hrec", [P, ORDER, L])
        h0 = [sb("h0_m", [P, ORDER]), sb("h0_t", [P, ORDER])]
        step_sb = sb("step_sb", [P, L])
        wout = [sb("wout_m_sb", [P, D]), sb("wout_t_sb", [P, D])]
        gate = [sb("gate_m_sb", [P, E]), sb("gate_t_sb", [P, E])]
        gateb_sb = sb("gateb_sb", [P, E])
        stat = sb("stat", [P, TILES, 2, 6])
        mv = sb("mv", [P, TILES, 2])
        std = sb("std", [P, TILES])
        rstd = sb("rstd", [P, TILES])
        nmr = sb("nmr", [P, TILES])
        h_tok = sb("h_tok", [P, TILES, D])
        u_tok = sb("u_tok", [P, TILES, D])
        x_all = sb("x_all", [P, 2, TILES * PD])
        xt = x_all[:, 0, :].rearrange("p (t n) -> p t n", t=TILES)
        xf = x_all[:, 1, :].rearrange("p (t c n) -> p t c n", t=TILES, c=FC)
        u = [sb("u_m", [P, HB, COLS]), sb("u_t", [P, 1, COLS])]
        v = [sb("v_m", [P, HB, COLS]), sb("v_t", [P, 1, COLS])]
        z = [sb("z_m", [P, HB, COLS]), sb("z_t", [P, 1, COLS])]
        x = [[sb(f"x{i}_m", [P, HB, COLS]), sb(f"x{i}_t", [P, 1, COLS])] for i in range(ORDER)]
        y = z
        mx = sb("mx", [P, TILES])
        sums = sb("sums", [P, TILES])
        cmb = sb("cmb", [P, TILES, NX])
        gs = sb("gs", [P, 14, TILES * E])
        gr = sb("gr", [P, 4, TILES])
        idx = sb("idx", [P, TILES * E])
        WEXP = 4 * I + IC * D
        wx = x_all[:, :, :].rearrange("p a n -> p (a n)")[:, 0:2 * WEXP].rearrange("p (s n) -> p s n", s=2)
        g_sb = sb("g_sb", [P, 2, 256])
        up_sb = sb("up_sb", [P, 2, 256])
        hT = sb("hT", [P, 2, IC, 256])

        s_id = sem("s_id"); s_small = sem("s_small"); s_xt = [sem(f"s_xt{h}") for h in range(HB)]; s_xf = [sem(f"s_xf{h}") for h in range(HB)]
        s_wx = [sem("s_w_even"), sem("s_w_odd")]
        s_out = sem("s_out")
        ones_set = sem("ones_set"); dve_c = sem("dve_c"); act_c = sem("act_c"); pool_c = sem("pool_c")
        wg_ready = sem("wg_ready"); win_exp = sem("win_exp"); hw_ready = sem("hw_ready"); habs_ready = sem("habs_ready")
        hsum_ready = sem("hsum_ready"); cols_ready = sem("cols_ready"); emb_ready = sem("emb_ready"); emb_read = sem("emb_read")
        var_ready = sem("var_ready"); std_ready = sem("std_ready"); utok_ready = sem("utok_ready")
        uT_ready = sem("uT_ready"); u_ready = sem("u_ready"); zps_ready = sem("zps_ready"); z_copied = sem("z_copied")
        tap2_ready = sem("tap2_ready"); taps_done = sem("taps_done"); xT_ready = sem("xT_ready"); max_ready = sem("max_ready")
        exp_done = sem("exp_done"); rec_ready = sem("rec_ready"); soft_ready = sem("soft_ready"); sT_ready = sem("sT_ready")
        s_copied = sem("s_copied"); v_ready = sem("v_ready"); wout_ready = sem("wout_ready"); o_ready = sem("o_ready")
        hb_ready = sem("hb_ready"); gate_ps = sem("gate_ps"); gexp = sem("gexp"); gln = sem("gln"); gsq = sem("gsq"); g1s = sem("g1s"); g2s = sem("g2s"); g3s = sem("g3s")
        cmb_ready = sem("cmb_ready"); gu_ready = sem("gu_ready"); silu_done = sem("silu_done"); up_read = sem("up_read"); h_ready = sem("h_ready")
        g_used = sem("g_used"); down_ready = sem("down_ready"); down_read = sem("down_read"); pos_ready = sem("pos_ready")
        nmx_ready = sem("nmx_ready"); idx_ready = sem("idx_ready")

        SMALL = 0
        block = ctx.enter_context(nc.Block())

        def bc(row, n):
            return row.to_broadcast(n)

        small = [(w_sb[:, :, :], w_in), (g1_sb[:, :], g1), (b1_sb[:, :], b1), (rows_sb[:, :, :], rows),
                 (pos_sb[:, :, :], pos), (cls_sb[:, :], cls), (wlin[0][:, :], wlin_m), (wlin[1][:, :], wlin_t),
                 (chan[0][:, :], chan_m), (chan[1][:, :], chan_t), (hp[0][:, :, :], hp_m), (hp[1][:, :, :], hp_t),
                 (step_sb[:, :], steps), (wout[0][:, :], wout_m), (wout[1][:, :], wout_t), (gate[0][:, :], gate_m),
                 (gate[1][:, :], gate_t), (gateb_sb[:, :], gate_b), (id_sb[:, :], ident)]
        NSMALL = 16 * len(small)

        def half(hb):
            return slice(64 * hb, 64 * hb + 64)

        blocks = [(hb, t, n) for hb in range(HB) for t, n in ((0, 2), (2, 2), (4, 1))]

        @block.sync
        def _(sp):
            for dst, src in small:
                sp.dma_start(dst, src).then_inc(s_small, 16)
            for hb in range(HB):
                ts = slice(hb * TH, (hb + 1) * TH)
                sp.dma_start(xt[:, ts, :], xtok[ts].rearrange("t p n -> p t n")).then_inc(s_xt[hb], 16)
                sp.dma_start(xf[:, ts, :, :].rearrange("p t c n -> p t (c n)"),
                             xfeat[ts].rearrange("t p c n -> p t (c n)")).then_inc(s_xf[hb], 16)
            sp.wait_ge(emb_ready, TILES)
            sp.wait_ge(var_ready, 2)
            for e in range(NX):
                if e >= 2:
                    sp.wait_ge(down_ready, (e - 1) * TILES)
                k = e % 2
                for n, w in enumerate((w1, w3)):
                    sp.dma_start(wx[:, k, 2 * n * I:(2 * n + 1) * I], w[e, 0:P, :]).then_inc(s_wx[k], 16)
                    for hb in range(HB):
                        sp.dma_start(wx[half(hb), k, (2 * n + 1) * I:(2 * n + 2) * I], w[e, P:D, :]).then_inc(s_wx[k], 16)
                sp.dma_start(wx[:, k, 4 * I:].rearrange("p (c n) -> p c n", c=IC),
                             w2[e].rearrange("(c p) n -> p c n", p=P)).then_inc(s_wx[k], 16)
            sp.wait_ge(down_read, NX * TILES)
            for hb in range(HB):
                for j in range(TH):
                    n = min(LT, L - j * LT)
                    sp.dma_start(out[hb * BH:(hb + 1) * BH, j * LT:j * LT + n, :].rearrange("b l e -> l b e"),
                                 h_tok[0:n * BH, hb * TH + j, :]).then_inc(s_out, 16)
            sp.wait_ge(s_out, 16 * TILES)

        @block.gpsimd
        def _(pool):
            chain = [0]

            def link(ins):
                chain[0] += 1
                ins.then_inc(pool_c, 1)
                pool.wait_ge(pool_c, chain[0])
            pool.memset(ones[:, :], 1.0).then_inc(ones_set, 1)
            link(pool.memset(cmb[:, :, E:NX], 1.0))
            pool.iota(idx[:, :], pattern=[[0, TILES], [-1, E]], base=E, channel_multiplier=0,
                      allow_small_or_imprecise_dtypes=True).then_inc(idx_ready, 1)
            pool.wait_ge(s_small, NSMALL)
            link(pool.tensor_tensor(cls_sb[:, :], cls_sb[:, :], pos_sb[0:BH, 0, :], ALU.add))
            pool.tensor_tensor(pos_sb[:, :, :], pos_sb[:, :, :],
                               rows_sb[:, 2:3, :].to_broadcast([P, TH, D]), ALU.add).then_inc(pos_ready, 1)
            pool.wait_ge(pos_ready, 1)
            pool.tensor_tensor(wout[0][:, 0:P], wout[0][:, 0:P], id_sb[:, :], ALU.add).then_inc(wout_ready, 1)
            pool.wait_ge(wout_ready, 1)
            pool.tensor_tensor(wout[1][0:64, P:D], wout[1][0:64, P:D], id_sb[0:64, 0:64], ALU.add).then_inc(wout_ready, 1)
            pool.wait_ge(wout_ready, 2)
            pool.tensor_tensor(wout[1][64:P, P:D], wout[1][64:P, P:D], id_sb[64:P, 64:P], ALU.add).then_inc(wout_ready, 1)

        @block.scalar
        def _(act):
            chain = [0]

            def link(ins):
                chain[0] += 1
                ins.then_inc(act_c, 1)
                act.wait_ge(act_c, chain[0])
            act.wait_ge(s_small, NSMALL)
            for k in range(2):
                act.activation(win[k][:, :], step_sb[:, :], ACT.Exp, scale=chan[k][:, C_ALPHA:C_ALPHA + 1]).then_inc(win_exp, 1)
            act.wait_ge(hw_ready, 2)
            for k in range(2):
                act.activation(habs[k][:, :, :], hp[k][:, :, :], ACT.Abs).then_inc(habs_ready, 1)

            def sqrt(n):
                for hb in range(HB):
                    act.wait_ge(var_ready, 2 * n + hb + 1)
                    act.activation(std[:, hb * TH:(hb + 1) * TH], std[:, hb * TH:(hb + 1) * TH], ACT.Sqrt).then_inc(std_ready, 1)

            sqrt(0)
            sqrt(1)
            sqrt(2)

            def copy_uT(n, m, t):
                for hb in range(HB):
                    act.wait_ge(uT_ready, 2 * n + hb + 1)
                    act.activation(m[:, hb, :], ps_flat[:, hb * 2048:hb * 2048 + COLS], ACT.Copy).then_inc(u_ready, 1)
                    act.activation(t[half(hb), 0, :], ps_flat[half(hb), hb * 2048 + 1024:hb * 2048 + 1024 + COLS], ACT.Copy).then_inc(u_ready, 1)

            copy_uT(0, u[0], u[1])
            k = 0
            for n, (part, dst) in enumerate(((2, v), (0, x[0]), (1, x[1]))):
                if n:
                    act.wait_ge(taps_done, 2 * n)
                for m in range(2):
                    for hb in range(HB if m == 0 else 1):
                        for s in range(2):
                            act.wait_ge(zps_ready, k + 1)
                            act.activation(z[m][:, hb, s * SPLIT:(s + 1) * SPLIT], ps[:, 5 + k % 3, 0:SPLIT], ACT.Identity,
                                           bias=chan[m][:, C_BLIN + part:C_BLIN + part + 1]).then_inc(z_copied, 1)
                            k += 1
                act.wait_ge(z_copied, k)
                for m in range(2):
                    act.activation(dst[m][:, :, :], z[m][:, :, :], ACT.Identity, bias=chan[m][:, C_CONVB + part:C_CONVB + part + 1],
                                   scale=chan[m][:, C_TAP + 3 * part + 2:C_TAP + 3 * part + 3]).then_inc(tap2_ready, 1)
            for i in range(ORDER):
                act.wait_ge(nmx_ready, i + 1)
                if i:
                    act.wait_ge(sT_ready, 1)
                for t in range(TILES):
                    act.activation(u_tok[:, t, :], ps_tok[:, t // TH, t % TH, 0:D], ACT.Exp, bias=mx[:, t:t + 1],
                                   accum_out=sums[:, t:t + 1]).then_inc(exp_done, 1)
                act.wait_ge(rec_ready, i + 1)
                for t in range(TILES):
                    act.activation(u_tok[:, t, :], u_tok[:, t, :], ACT.Copy, scale=sums[:, t:t + 1]).then_inc(soft_ready, 1)
                act.wait_ge(sT_ready, i + 1)
                act.activation(x[i][0][:, :, :].rearrange("p h n -> p (h n)"), ps_flat[:, 0:HB * COLS], ACT.Copy).then_inc(s_copied, 1)
                for hb in range(HB):
                    act.activation(x[i][1][half(hb), 0, :],
                                   ps_flat[half(hb), HB * COLS + hb * COLS:HB * COLS + (hb + 1) * COLS], ACT.Copy).then_inc(s_copied, 1)
            sqrt(3)
            copy_uT(1, u[0], u[1])
            act.wait_ge(g1s, 1)
            act.activation(gs[:, 1, :], gs[:, 0, :], ACT.Exp, scale=-1.0).then_inc(gexp, 1)
            act.wait_ge(g2s, 1)
            act.activation(gs[:, 3, :], gs[:, 2, :], ACT.Ln).then_inc(gln, 1)
            act.wait_ge(g3s, 1)
            act.activation(gs[:, 5, :], gs[:, 4, :], ACT.Sqrt).then_inc(gsq, 1)
            k = 0
            for e in range(NX):
                for hb, t0, nt in blocks:
                    for c in range(IC):
                        act.wait_ge(gu_ready, k + 1)
                        if k >= 2:
                            act.wait_ge(h_ready, k - 1)
                        act.activation(g_sb[:, k % 2, 0:nt * P], ps[:, k % 2, 0:nt * P], ACT.Silu).then_inc(silu_done, 1)
                        k += 1

        @block.vector
        def _(dve):
            chain = [0]

            def link(ins):
                chain[0] += 1
                ins.then_inc(dve_c, 1)
                dve.wait_ge(dve_c, chain[0])

            vr = [0]

            def norm_stats(src, hb, width, n):
                t0 = hb * TH
                for t in range(t0, t0 + TH):
                    if n == 0:
                        dve.wait_ge(s_xt[hb], 16)
                    for k in range(width // 384 if width > 384 else 1):
                        w = min(width, 384)
                        link(dve.bn_stats(stat[:, t, k, :], src[:, t, k * w:(k + 1) * w]))
                    nk = 2 if width > 384 else 1
                    link(dve.bn_aggr(mv[:, t, :], stat[:, t, 0:nk, :]))
                dve.tensor_scalar(std[:, t0:t0 + TH], mv[:, t0:t0 + TH, 1], EPS, None, ALU.add).then_inc(var_ready, 1)

            def norm_scale(hb, n):
                t0 = hb * TH
                dve.wait_ge(std_ready, 2 * n + hb + 1)
                link(dve.reciprocal(rstd[:, t0:t0 + TH], std[:, t0:t0 + TH]))

            dve.wait_ge(s_small, NSMALL)
            dve.wait_ge(ones_set, 1)
            for c in range(FC):
                dve.tensor_scalar(wg_sb[:, c, :], w_sb[:, c, :], g1_sb[:, c:c + 1], None, ALU.mult).then_inc(wg_ready, 1)
                dve.tensor_scalar(b1_wide[:, c, :], ones[:, :], b1_sb[:, c:c + 1], None, ALU.mult).then_inc(wg_ready, 1)
            dve.wait_ge(win_exp, 2)
            for k in range(2):
                link(dve.tensor_scalar(win[k][:, :], win[k][:, :], chan[k][:, C_WINB:C_WINB + 1], None, ALU.add))
                dve.tensor_tensor(hp[k][:, :, :], hp[k][:, :, :], win[k][:, :].rearrange("p (a n) -> p a n", a=1).to_broadcast([P, ORDER, L]),
                                  ALU.mult).then_inc(hw_ready, 1)
            norm_stats(xt, 0, PD, 0)
            dve.wait_ge(hsum_ready, 1)
            link(dve.reciprocal(hrec[:, :, :], ps[:, 7, 0:ORDER * L].rearrange("p (o l) -> p o l", o=ORDER)))
            for k in range(2):
                link(dve.tensor_tensor(hp[k][:, :, :], hp[k][:, :, :], hrec[:, :, :], ALU.mult))
                link(dve.tensor_tensor(h0[k][:, :], hp[k][:, :, 0], chan[k][:, C_BMAT:C_BMAT + ORDER], ALU.add))
            dve.wait_ge(cols_ready, 1)
            link(dve.tensor_copy(colsum[:, :], ps[:, 6, 0:D]))
            link(dve.tensor_tensor(shift[:, :], ps[:, 6, 256:256 + D], rows_sb[:, 0, :], ALU.add))
            norm_stats(xt, 1, PD, 0)
            for hb in range(HB):
                t0 = hb * TH
                ts = slice(t0, t0 + TH)
                norm_scale(hb, 0)
                link(dve.scalar_tensor_tensor(out=nmr[:, ts], in0=mv[:, ts, 0], scalar=-1.0, in1=rstd[:, ts], op0=ALU.mult, op1=ALU.mult))
                dve.wait_ge(emb_ready, t0 + TH)
                for t in range(t0, t0 + TH):
                    dve.tensor_scalar(u_tok[:, t, :], ps_tok[:, t // TH, t % TH, 0:D], rstd[:, t:t + 1], None, ALU.mult).then_inc(emb_read, 1)
                dve.wait_ge(emb_read, t0 + TH)
                for t in range(t0, t0 + TH):
                    link(dve.scalar_tensor_tensor(out=u_tok[:, t, :], in0=colsum[:, :], scalar=nmr[:, t:t + 1], in1=u_tok[:, t, :], op0=ALU.mult, op1=ALU.add))
                sh = shift[:, :].rearrange("p (a n) -> p a n", a=1).to_broadcast([P, TH, D])
                link(dve.tensor_tensor(u_tok[:, ts, :], u_tok[:, ts, :], sh, ALU.add))
                norm_stats(u_tok, hb, D, 1)
            for hb in range(HB):
                t0 = hb * TH
                ts = slice(t0, t0 + TH)
                norm_scale(hb, 1)
                for t in range(t0, t0 + TH):
                    link(dve.tensor_scalar(h_tok[:, t, :], u_tok[:, t, :], mv[:, t, 0:1], rstd[:, t:t + 1], ALU.subtract, ALU.mult))
                link(dve.tensor_tensor(h_tok[:, ts, :], h_tok[:, ts, :], rows_sb[:, 1:2, :].to_broadcast([P, TH, D]), ALU.mult))
                dve.wait_ge(pos_ready, 1)
                link(dve.tensor_tensor(h_tok[:, ts, :], h_tok[:, ts, :], pos_sb[:, :, :], ALU.add))
                link(dve.tensor_copy(h_tok[0:BH, t0, :], cls_sb[:, :]))
                norm_stats(h_tok, hb, D, 2)
            for hb in range(HB):
                t0 = hb * TH
                ts = slice(t0, t0 + TH)
                norm_scale(hb, 2)
                for t in range(t0, t0 + TH):
                    dve.tensor_scalar(u_tok[:, t, :], h_tok[:, t, :], mv[:, t, 0:1], rstd[:, t:t + 1], ALU.subtract, ALU.mult).then_inc(utok_ready, 1)
                dve.wait_ge(utok_ready, t0 + TH)
                link(dve.tensor_tensor(h_tok[:, ts, :], h_tok[:, ts, :], rows_sb[:, 3:4, :].to_broadcast([P, TH, D]), ALU.add))
            for n, (part, dst) in enumerate(((2, v), (0, x[0]), (1, x[1]))):
                dve.wait_ge(tap2_ready, 2 * n + 2)
                for m in range(2):
                    for back in (1, 2):
                        o = back * BH
                        tap = chan[m][:, C_TAP + 3 * part + 2 - back:C_TAP + 3 * part + 3 - back]
                        ins = dve.scalar_tensor_tensor(out=dst[m][:, :, o:], in0=z[m][:, :, 0:COLS - o], scalar=tap,
                                                       in1=dst[m][:, :, o:], op0=ALU.mult, op1=ALU.add)
                        if back == 1:
                            link(ins)
                        else:
                            ins.then_inc(taps_done, 1)
                dve.wait_ge(taps_done, 2 * n + 2)
                if part == 2:
                    for m in range(2):
                        link(dve.tensor_tensor(v[m][:, :, :], v[m][:, :, :], u[m][:, :, :], ALU.add))
            for i in range(ORDER):
                dve.wait_ge(xT_ready, i + 1)
                link(dve.tensor_reduce(mx[:, :].rearrange("p (h t) -> p h t", h=HB), ps_tok[:, :, 0:TH, 0:D], AX.X, ALU.max))
                dve.tensor_scalar(mx[:, :], mx[:, :], -1.0, None, ALU.mult).then_inc(nmx_ready, 1)
                for m in range(2):
                    link(dve.tensor_scalar(y[m][:, :, 0:REAL], v[m][:, :, 0:REAL], h0[m][:, i:i + 1], None, ALU.mult))
                for j in range(1, L):
                    o = j * BH
                    if j == 8:
                        dve.wait_ge(exp_done, TILES * (i + 1))
                        dve.reciprocal(sums[:, :], sums[:, :]).then_inc(rec_ready, 1)
                    for m in range(2):
                        link(dve.scalar_tensor_tensor(out=y[m][:, :, o:REAL], in0=v[m][:, :, 0:REAL - o], scalar=hp[m][:, i, j:j + 1],
                                                      in1=y[m][:, :, o:REAL], op0=ALU.mult, op1=ALU.add))
                dve.wait_ge(s_copied, 3 * (i + 1))
                for m in range(2):
                    link(dve.tensor_tensor(y[m][:, :, 0:REAL], y[m][:, :, 0:REAL], x[i][m][:, :, 0:REAL], ALU.mult))
                    dve.tensor_tensor(v[m][:, :, 0:REAL], v[m][:, :, 0:REAL], y[m][:, :, 0:REAL], ALU.add).then_inc(v_ready, 1)
                dve.wait_ge(v_ready, 2 * (i + 1))
            for hb in range(HB):
                t0 = hb * TH
                ts = slice(t0, t0 + TH)
                dve.wait_ge(o_ready, (hb + 1) * TH)
                link(dve.tensor_tensor(h_tok[:, ts, :], h_tok[:, ts, :], ps_tok[:, hb, 0:TH, 0:D], ALU.add))
                norm_stats(h_tok, hb, D, 3)
            for hb in range(HB):
                t0 = hb * TH
                norm_scale(hb, 3)
                for t in range(t0, t0 + TH):
                    dve.tensor_scalar(u_tok[:, t, :], h_tok[:, t, :], mv[:, t, 0:1], rstd[:, t:t + 1], ALU.subtract, ALU.mult).then_inc(utok_ready, 1)
            dve.wait_ge(gate_ps, 1)
            G = gs
            link(dve.tensor_copy(G[:, 6, :].rearrange("p (h n) -> p h n", h=HB), ps[:, 6:8, 0:TH * E]))
            link(dve.tensor_scalar(G[:, 7, :], G[:, 6, :], -1.0, None, ALU.mult))
            dve.tensor_tensor(G[:, 0, :], G[:, 6, :], G[:, 7, :], ALU.max).then_inc(g1s, 1)
            dve.wait_ge(gexp, 1)
            dve.tensor_scalar(G[:, 2, :], G[:, 1, :], 1.0, None, ALU.add).then_inc(g2s, 1)
            dve.wait_ge(g2s, 1)
            link(dve.tensor_scalar(G[:, 8, :], G[:, 2, :], 1.0, None, ALU.subtract))
            link(dve.tensor_scalar(G[:, 9, :], G[:, 8, :], 0.0, None, ALU.is_equal))
            link(dve.tensor_tensor(G[:, 8, :], G[:, 8, :], G[:, 9, :], ALU.add))
            link(dve.reciprocal(G[:, 8, :], G[:, 8, :]))
            link(dve.tensor_tensor(G[:, 8, :], G[:, 8, :], G[:, 1, :], ALU.mult))
            dve.wait_ge(gln, 1)
            link(dve.tensor_tensor(G[:, 3, :], G[:, 3, :], G[:, 9, :], ALU.max))
            link(dve.tensor_tensor(G[:, 3, :], G[:, 3, :], G[:, 8, :], ALU.mult))
            dve.scalar_tensor_tensor(out=G[:, 4, :], in0=G[:, 6, :], scalar=0.0, in1=G[:, 3, :], op0=ALU.max, op1=ALU.add).then_inc(g3s, 1)
            dve.wait_ge(gsq, 1)
            dve.wait_ge(idx_ready, 1)

            def v3(k):
                return G[:, k, :].rearrange("p (t e) -> p t e", e=E)

            def over(k):
                return gr[:, k, :].rearrange("p (t a) -> p t a", a=1).to_broadcast([P, TILES, E])
            link(dve.tensor_tensor(v3(6), v3(5), gateb_sb[:, :].rearrange("p (a e) -> p a e", a=1).to_broadcast([P, TILES, E]), ALU.add))
            for k in range(2):
                link(dve.tensor_reduce(gr[:, k, :], v3(6), AX.X, ALU.max))
                link(dve.tensor_tensor(v3(7), v3(6), over(k), ALU.is_equal))
                link(dve.tensor_tensor(G[:, 7, :], G[:, 7, :], idx[:, :], ALU.mult))
                link(dve.tensor_reduce(gr[:, 2, :], v3(7), AX.X, ALU.max))
                link(dve.tensor_tensor(v3(10 + k), v3(7), over(2), ALU.is_equal))
                if k == 0:
                    link(dve.scalar_tensor_tensor(out=G[:, 6, :], in0=G[:, 10, :], scalar=-1e30, in1=G[:, 6, :], op0=ALU.mult, op1=ALU.add))
            link(dve.tensor_tensor(G[:, 10, :], G[:, 10, :], G[:, 11, :], ALU.add))
            link(dve.tensor_tensor(G[:, 10, :], G[:, 10, :], G[:, 5, :], ALU.mult))
            link(dve.tensor_reduce(gr[:, 2, :], v3(10), AX.X, ALU.add))
            link(dve.tensor_scalar(gr[:, 2, :], gr[:, 2, :], 1e-6, None, ALU.max))
            link(dve.reciprocal(gr[:, 3, :], gr[:, 2, :]))
            link(dve.tensor_tensor(cmb[:, :, 0:E], v3(10), over(3), ALU.mult))
            k = 0
            nd = 0
            for e in range(NX):
                for b, (hb, t0, nt) in enumerate(blocks):
                    q = (e * len(blocks) + b) % 2
                    for c in range(IC):
                        dve.wait_ge(gu_ready, k + 1)
                        dve.tensor_scalar(up_sb[:, k % 2, 0:nt * P], ps[:, 2 + k % 2, 0:nt * P], LIMIT, -LIMIT, ALU.min, ALU.max).then_inc(up_read, 1)
                        dve.wait_ge(up_read, k + 1)
                        dve.wait_ge(silu_done, k + 1)
                        if c == 0 and e * len(blocks) + b >= 2:
                            pb = e * len(blocks) + b - 2
                            dve.wait_ge(down_ready, sum(blocks[i % len(blocks)][2] for i in range(pb + 1)))
                        dve.scalar_tensor_tensor(out=hT[:, q, c, 0:nt * P], in0=g_sb[:, k % 2, 0:nt * P], scalar=SILU_LIMIT,
                                                 in1=up_sb[:, k % 2, 0:nt * P], op0=ALU.min, op1=ALU.mult).then_inc(h_ready, 1)
                        k += 1
                    for t in range(t0, t0 + nt):
                        ti = hb * TH + t
                        dve.wait_ge(down_ready, nd + 1)
                        dve.wait_ge(down_read, nd) if nd else None
                        dve.scalar_tensor_tensor(out=h_tok[:, ti, :], in0=ps[:, 4 + nd % 4, 0:D], scalar=cmb[:, ti, e:e + 1],
                                                 in1=h_tok[:, ti, :], op0=ALU.mult, op1=ALU.add).then_inc(down_read, 1)
                        nd += 1

        @block.tensor
        def _(pe):
            def mm(o, lhsT, rhs, first, last):
                return pe.matmul(o, lhsT, rhs, start=first, stop=last, skip_group_check=True)

            pe.wait_ge(s_small, NSMALL)
            pe.wait_ge(ones_set, 1)
            pe.wait_ge(wg_ready, 2 * FC)
            for c in range(FC):
                mm(ps[:, 6, 0:D], ones[:, :], wg_sb[:, c, :], c == 0, c == FC - 1)
            for c in range(FC):
                last = mm(ps[:, 6, 256:256 + D], b1_wide[:, c, :], w_sb[:, c, :], c == 0, c == FC - 1)
            last.then_inc(cols_ready, 1)
            pe.wait_ge(habs_ready, 2)
            mm(ps[:, 7, 0:ORDER * L], ones[:, :], habs[0][:, :, :].rearrange("p o l -> p (o l)"), True, False)
            mm(ps[:, 7, 0:ORDER * L], ones[0:64, :], habs[1][0:64, :, :].rearrange("p o l -> p (o l)"), False, True).then_inc(hsum_ready, 1)
            for t in range(TILES):
                pe.wait_ge(s_xf[t // TH], 16)
                for c in range(FC):
                    last = mm(ps_tok[:, t // TH, t % TH, 0:D], xf[:, t, c, :], wg_sb[:, c, :], c == 0, c == FC - 1)
                last.then_inc(emb_ready, 1)
            pe.wait_ge(emb_ready, TILES)

            def transpose_tail(hb, o, t):
                if hb == 0:
                    return pe.transpose(ps_flat[0:DT, o:o + P], u_tok[:, t, P:D], id_sb[:, :])
                return pe.transpose(ps_flat[:, o:o + P], u_tok[:, t, D - P:D], id_sb[:, :])

            def transpose_u(n):
                for hb in range(HB):
                    for j in range(TH):
                        t = hb * TH + j
                        pe.wait_ge(utok_ready, n * TILES + t + 1)
                        o = hb * 2048 + j * P
                        pe.transpose(ps_flat[:, o:o + P], u_tok[:, t, 0:P], id_sb[:, :])
                        last = transpose_tail(hb, o + 1024, t)
                    last.then_inc(uT_ready, 1)

            pe.wait_ge(emb_read, TILES)
            transpose_u(0)
            pe.wait_ge(u_ready, 4)
            k = 0

            def project(part):
                nonlocal k
                c0 = part * D
                for m in range(2):
                    for hb in range(HB if m == 0 else 1):
                        for s in range(2):
                            if k >= 3:
                                pe.wait_ge(z_copied, k - 2)
                            cs = slice(s * SPLIT, (s + 1) * SPLIT)
                            if m == 0:
                                o = ps[:, 5 + k % 3, 0:SPLIT]
                                mm(o, wlin[0][:, c0:c0 + P], u[0][:, hb, cs], True, False)
                                last = mm(o, wlin[1][half(hb), c0:c0 + P], u[1][half(hb), 0, cs], False, True)
                            else:
                                for h in range(HB):
                                    o = ps[half(h), 5 + k % 3, 0:SPLIT]
                                    mm(o, wlin[0][:, c0 + P:c0 + D], u[0][:, h, cs], True, False)
                                    last = mm(o, wlin[1][half(h), c0 + P:c0 + D], u[1][half(h), 0, cs], False, True)
                            last.then_inc(zps_ready, 1)
                            k += 1

            def to_tokens(i):
                for t in range(TILES):
                    hb, j = divmod(t, TH)
                    cs = slice(j * P, (j + 1) * P)
                    pe.transpose(ps_tok[:, hb, j, 0:P], x[i][0][:, hb, cs], id_sb[:, :])
                    last = pe.transpose(ps_tok[:, hb, j, P:D], x[i][1][half(hb), 0, cs], id_sb[half(hb), half(hb)])
                last.then_inc(xT_ready, 1)

            def to_channels(i):
                for t in range(TILES):
                    pe.wait_ge(soft_ready, i * TILES + t + 1)
                    pe.transpose(ps_flat[:, t * P:(t + 1) * P], u_tok[:, t, :][:, 0:P], id_sb[:, :])
                    o = HB * COLS + t * P
                    last = transpose_tail(t // TH, o, t)
                last.then_inc(sT_ready, 1)

            project(2)
            project(0)
            project(1)
            pe.wait_ge(taps_done, 4)
            pe.wait_ge(z_copied, k)
            to_tokens(0)
            to_channels(0)
            pe.wait_ge(taps_done, 6)
            pe.wait_ge(s_copied, 3)
            to_tokens(1)
            to_channels(1)
            pe.wait_ge(v_ready, 4)
            pe.wait_ge(s_copied, 6)
            pe.wait_ge(wout_ready, 3)
            for t in range(TILES):
                hb, j = divmod(t, TH)
                cs = slice(j * P, (j + 1) * P)
                mm(ps_tok[:, t // TH, t % TH, 0:D], v[0][:, hb, cs], wout[0][:, :], True, False)
                mm(ps_tok[:, t // TH, t % TH, 0:D], v[1][half(hb), 0, cs], wout[1][half(hb), :], False, True).then_inc(o_ready, 1)
            pe.wait_ge(var_ready, 8)
            transpose_u(1)
            pe.wait_ge(u_ready, 8)
            for t in range(TILES):
                hb, j = divmod(t, TH)
                cs = slice(j * P, (j + 1) * P)
                mm(ps[:, 6 + hb, j * E:(j + 1) * E], u[0][:, hb, cs], gate[0][:, :], True, False)
                last = mm(ps[:, 6 + hb, j * E:(j + 1) * E], u[1][half(hb), 0, cs], gate[1][half(hb), :], False, True)
            last.then_inc(gate_ps, 1)
            k = 0
            nd = 0
            for e in range(NX):
                s = e % 2
                pe.wait_ge(s_wx[s], 16 * 7 * (e // 2 + 1))
                for b, (hb, t0, nt) in enumerate(blocks):
                    q = (e * len(blocks) + b) % 2
                    cs = slice(t0 * P, (t0 + nt) * P)
                    for c in range(IC):
                        if k >= 2:
                            pe.wait_ge(h_ready, k - 1)
                        for n in range(2):
                            o = ps[:, 2 * n + k % 2, 0:nt * P]
                            wm = wx[:, s, 2 * n * I + c * P:2 * n * I + (c + 1) * P]
                            wt = wx[half(hb), s, (2 * n + 1) * I + c * P:(2 * n + 1) * I + (c + 1) * P]
                            mm(o, wm, u[0][:, hb, cs], True, False)
                            last = mm(o, wt, u[1][half(hb), 0, cs], False, True)
                        last.then_inc(gu_ready, 1)
                        k += 1
                    pe.wait_ge(h_ready, k)
                    for t in range(nt):
                        if nd >= 4:
                            pe.wait_ge(down_read, nd - 3)
                        for c in range(IC):
                            last = mm(ps[:, 4 + nd % 4, 0:D], hT[:, q, c, t * P:(t + 1) * P],
                                      wx[:, s, 4 * I + c * D:4 * I + (c + 1) * D], c == 0, c == IC - 1)
                        last.then_inc(down_ready, 1)
                        nd += 1


def kernel(**inputs):
    import numpy as np
    import concourse.bacc as bacc
    from concourse.bass_utils import run_bass_kernel_spmd

    a = {k: np.ascontiguousarray(v) for k, v in inputs.items()}
    f32 = np.float32

    def tiles(m):
        n = m.shape[2]
        padded = np.zeros((HB, LP, BH, n), f32)
        padded[:, :m.shape[1]] = m.reshape(HB, BH, m.shape[1], n).transpose(0, 2, 1, 3)
        return padded.reshape(TILES, P, n)

    def wide(row):
        return np.ascontiguousarray(np.broadcast_to(row, (P,) + row.shape))

    def split(m):
        return np.ascontiguousarray(m[:P]), np.concatenate([m[P:], m[P:]])

    patches = a["x"].reshape(B, 3, 6, 16, 6, 16).transpose(0, 2, 4, 3, 5, 1).reshape(B, 36, PD)
    patches = np.concatenate([np.zeros((B, 1, PD), f32), patches], axis=1)
    xtok = tiles(patches)
    pos = np.zeros((LP, D), f32)
    pos[:L] = a["L0_tok_pos_embed"][0]
    chan = np.concatenate([a["L0_attn_b_lin"].reshape(3, D).T,
                           a["L0_attn_conv_w"].reshape(3, D, 3).transpose(1, 0, 2).reshape(D, 9),
                           a["L0_attn_conv_b"].reshape(3, D).T, a["L0_attn_alphas"].reshape(D, 1),
                           a["L0_attn_win_b"].reshape(D, 1), a["L0_attn_Bmat"].reshape(ORDER, D).T], axis=1)
    ins = {
        "xtok": xtok,
        "xfeat": xtok.reshape(TILES, P, FC, P).transpose(0, 3, 2, 1),
        "pos": pos.reshape(TH, LT, 1, D).repeat(BH, 2).reshape(TH, P, D).transpose(1, 0, 2),
        "ident": np.eye(P, dtype=f32),
        "steps": wide(np.linspace(0.0, 1.0, 512, dtype=f32)[:L]),
        "w_in": a["L0_tok_W"].reshape(FC, P, D).transpose(1, 0, 2),
        "g1": a["L0_tok_ln1_g"].reshape(FC, P).T,
        "b1": a["L0_tok_ln1_b"].reshape(FC, P).T,
        "rows": wide(np.stack([a["L0_tok_b"], a["L0_tok_ln2_g"], a["L0_tok_ln2_b"], a["L0_attn_b_out"]])),
        "cls": np.broadcast_to(a["L0_tok_cls_token"], (BH, D)),
    }
    ins["wlin_m"], ins["wlin_t"] = split(a["L0_attn_W_lin"].T)
    ins["chan_m"], ins["chan_t"] = split(chan)
    ins["hp_m"], ins["hp_t"] = split(a["L0_attn_h_param"].transpose(1, 0, 2)[:, :, :L])
    ins["wout_m"], ins["wout_t"] = split(a["L0_attn_W_out"].T)
    ins["gate_m"], ins["gate_t"] = split(a["L0_ffn_gate_w"])
    ins["gate_b"] = wide(a["L0_ffn_gate_bias"])
    for n in ("w1", "w3", "w2"):
        ins[n] = np.concatenate([a["L0_ffn_" + n], a["L0_ffn_" + n + "s"][None]])

    nc = bacc.Bacc("TRN2", target_bir_lowering=False, num_devices=1)
    arrays, args = {}, []
    for name, m in ins.items():
        arrays["in_" + name] = np.ascontiguousarray(m)
        args.append(nc.dram_tensor("in_" + name, m.shape, F32, kind="ExternalInput").ap())
    args.append(nc.dram_tensor("out_0", (B, L, D), F32, kind="ExternalOutput").ap())
    build(nc, *args)
    r = run_bass_kernel_spmd(nc, [arrays], core_ids=[0])
    return r.results[0]["out_0"]
```

```python
from contextlib import ExitStack

import concourse.bass as bass
from concourse import mybir

ALU = mybir.AluOpType
ACT = mybir.ActivationFunctionType
F32 = mybir.dt.float32
F16 = mybir.dt.float16
I32 = mybir.dt.int32
AX = mybir.AxisListType

P = 128
B = 32
HB = 2
BH = B // HB
L = 37
LT = P // BH
TH = -(-L // LT)
LP = TH * LT
TILES = HB * TH
COLS = LP * BH
REAL = L * BH
PD = 768
FC = PD // P
D = 192
DT = D - P
ORDER = 2
PE_LAGS = (6, 9)
CB = REAL // 2
E = 8
I = 768
IC = I // P
EPS = 1e-5
LIMIT = 10.0
SILU_LIMIT = 9.999546021312975
SPLIT = COLS // 2
TOPK = 2
NX = E + 1
HI = I // 2
ROUTED = (TOPK * B * L + E * (P - 1)) // P
NT = TILES + ROUTED
PAIRS = NT // 2
SHARED_PAIRS = TILES // 2
assert NT % 2 == 0 and TILES % 2 == 0
ROW = 4 * P
SLOT = 6 * I + 2 * IC * D
W2_AT = 6 * I
CHUNKS = 3
CHUNK = 2 * I
RING = 3
KEPT = 5
C_BLIN, C_TAP, C_CONVB, C_ALPHA, C_WINB, C_BMAT = 0, 3, 12, 15, 16, 17
NCH = C_BMAT + ORDER
T_REAL, T_DOWN = 0, TILES
T_FULL, T_TILE = T_DOWN + TILES * E, T_DOWN + TILES * E + TILES
NTAB = T_TILE + (2 * B * L + E * (P - 1)) // P


def build(nc, xtok, xfeat, pos, ident, steps, w_in, g1, b1, rows, cls, wlin_m, wlin_t, chan_m, chan_t,
          hp_m, hp_t, wout_m, wout_t, gate_m, gate_t, gate_b, tables, upper, w1, w3, w2, out):
    with ExitStack() as ctx:
        def sb(name, shape, dt=F32):
            return ctx.enter_context(nc.sbuf_tensor(name, shape, dt))

        def sem(name):
            return ctx.enter_context(nc.semaphore(name))

        ps = ctx.enter_context(nc.psum_tensor("ps", [P, 8, 512], F32))
        ps_tok = ps[:, 0:6, :].rearrange("p (a b) (h n) -> p a (b h) n", a=HB, h=2)
        ps_flat = ps[:, :, :].rearrange("p b n -> p (b n)")

        def psum16(bank, n):
            return ps[:, bank, 0:n // 2].bitcast(F16)

        def cut(tensor, dt=F32):
            at = [0]

            def take(*shape, dtype=F32):
                n = 1
                for k in shape:
                    n *= k
                words = n // 2 if dtype == F16 else n
                view = tensor[:, at[0]:at[0] + words]
                at[0] += words
                assert at[0] <= tensor.shape[1], (at[0], tensor.shape)
                if dtype == F16:
                    view = view.bitcast(F16)
                if len(shape) == 1:
                    return view
                names = "abcd"[:len(shape)]
                return view.rearrange(f"p ({' '.join(names)}) -> p {' '.join(names)}", **dict(zip(names, shape)))
            return take

        id_sb = sb("id_sb", [P, P])
        id16 = sb("id16", [P, P], F16)
        ones = sb("ones", [P, P])
        zeros = sb("zeros", [P, ROW], F16)
        g1_sb = sb("g1_sb", [P, FC])
        b1_sb = sb("b1_sb", [P, FC])
        rows_sb = sb("rows_sb", [P, 4, D])
        cls_sb = sb("cls_sb", [BH, D])
        chan = [sb("chan_m_sb", [P, NCH]), sb("chan_t_sb", [P, NCH])]
        hp = [sb("hp_m_sb", [P, ORDER, L]), sb("hp_t_sb", [P, ORDER, L])]
        habs = [sb("habs_m", [P, ORDER, L]), sb("habs_t", [P, ORDER, L])]
        win = [sb("win_m", [P, L]), sb("win_t", [P, L])]
        hrec = sb("hrec", [P, ORDER, L])
        h0 = [sb("h0_m", [P, ORDER]), sb("h0_t", [P, ORDER])]
        step_sb = sb("step_sb", [P, L])
        gate = [sb("gate_m_sb", [P, E]), sb("gate_t_sb", [P, E])]
        gateb_sb = sb("gateb_sb", [P, E])
        stat = sb("stat", [P, TILES, 2, 6])
        mv = sb("mv", [P, TILES, 2])
        std = sb("std", [P, TILES])
        rstd = sb("rstd", [P, TILES])
        nmr = sb("nmr", [P, TILES])
        h_tok = sb("h_tok", [P, TILES, D])
        u_tok = sb("u_tok", [P, TILES, D])
        mx = sb("mx", [P, ORDER, TILES])
        sums = sb("sums", [P, ORDER, TILES])
        gs = sb("gs", [P, 14, TILES * E])
        gr = sb("gr", [P, 4, TILES])
        tab = sb("tab", [P, NTAB])
        upper_sb = sb("upper_sb", [P, P])
        run = sb("run", [P, TILES + 1, E])
        tiles_of = sb("tiles_of", [P, E])
        first_tile = sb("first_tile", [P, E + 1])
        scratch = sb("scratch", [P, ROUTED * E])
        wk = sb("wk", [P, TOPK, TILES])
        slot_f = sb("slot_f", [P, TOPK, TILES])
        slot_i = sb("slot_i", [P, TOPK, TILES], I32)
        place_f = sb("place_f", [1, NT])
        place_i = sb("place_i", [1, NT], I32)
        slots = sb("slots", [P, NX * SLOT // 2])
        w16 = slots[:, :].bitcast(F16)
        stage = sb("stage", [P, RING, CHUNK])
        LATE = 3
        take = cut(slots[:, (NX - LATE) * SLOT // 2:])
        u = [take(HB, COLS), take(1, COLS)]
        v = [take(HB, COLS), take(1, COLS)]
        z = [take(HB, COLS), take(1, COLS)]
        x = [[take(HB, COLS), take(1, COLS)] for _ in range(ORDER)]
        y = z
        x_at = (NX - LATE) * SLOT // 2 + 9 * COLS
        x_tok = [slots[:, x_at + 3 * COLS * i:x_at + 3 * COLS * (i + 1)].rearrange("p (t n) -> p t n", t=TILES) for i in range(ORDER)]
        u_flat = u_tok[:, :, :].rearrange("p t n -> p (t n)")
        soft = [[u_flat[:, 0:HB * COLS].rearrange("p (h n) -> p h n", h=HB),
                 u_flat[:, HB * COLS:].rearrange("p (h n) -> p h n", h=1)], x[0]]
        take = cut(slots[:, (NX - LATE) * SLOT // 2 + 3 * COLS:])
        xt = take(KEPT, PD)
        xf = take(KEPT, FC, P)
        gathered = slots[:, 0:TILES * TOPK * D].rearrange("p (t k n) -> p t k n", t=TILES, k=TOPK)
        front = sb("front", [P, 8832])
        take = cut(front)
        w_sb = take(FC, D)
        wg_sb = take(FC, D)
        b1_wide = take(FC, P)
        pos_sb = take(TH, D)
        colsum = take(D)
        shift = take(D)
        wlin = [take(3 * D), take(3 * D)]
        wout = [take(D), take(D)]
        diag = [take(2, PE_LAGS[0], P)]
        diag.append(cut(front)(2, PE_LAGS[1], P))
        take = cut(front)
        xr = take(TILES, ROW, dtype=F16)
        xs = take(2, ROW, dtype=F16)
        xT = take(2, 4, P, dtype=F16)
        sg = take(2, HI)
        uc = take(2, HI)
        hid = take(2, HI)
        hhl = take(2, 2, HI, dtype=F16)
        hT = take(2, 2, 2 * HI, dtype=F16)
        ybuf = take(2, D)
        shared_y = u_tok
        x_rows = nc.dram_tensor("x_rows", [NT * P, ROW], F16).ap()
        y_rows = nc.dram_tensor("y_rows", [NT * P, D], F32).ap()

        names = """s_small s_front s_out ones_set dve_c act_c pool_c wg_ready win_exp hw_ready habs_ready hsum_ready
            cols_ready emb_ready emb_read var_ready std_ready utok_ready uT_ready u_ready zps_ready z_copied
            tap2_ready taps_done xT_ready exp_done rec_ready soft_ready sT_ready s_copied v_ready
            wout_ready o_ready gate_ps gexp gln gsq g1s g2s g3s pos_ready nmx_ready
            zero_set zero_out stats_done xhi_ready xlo_ready s_rows m_ready pre_ready slots_ready place_ready s_scatter
            hi_split lo_split tail_split w_part split_all x_turned x_copied up_done silu_done clip_done h_ready hi_done lo_done h_turned ha_copied
            hb_copied down_done y_copied s_shared summed id16_set diag_ready v_base conv_ready s_turned taps_of_u h0_ready""".split()
        S = {n: sem(n) for n in names}
        (s_small, s_front, s_out, ones_set, dve_c, act_c, pool_c, wg_ready, win_exp, hw_ready, habs_ready, hsum_ready,
         cols_ready, emb_ready, emb_read, var_ready, std_ready, utok_ready, uT_ready, u_ready, zps_ready, z_copied,
         tap2_ready, taps_done, xT_ready, exp_done, rec_ready, soft_ready, sT_ready, s_copied, v_ready,
         wout_ready, o_ready, gate_ps, gexp, gln, gsq, g1s, g2s, g3s, pos_ready, nmx_ready,
         zero_set, zero_out, stats_done, xhi_ready, xlo_ready, s_rows, m_ready, pre_ready, slots_ready, place_ready, s_scatter,
         hi_split, lo_split, tail_split, w_part, split_all, x_turned, x_copied, up_done, silu_done, clip_done, h_ready, hi_done, lo_done, h_turned, ha_copied,
         hb_copied, down_done, y_copied, s_shared, summed, id16_set, diag_ready, v_base, conv_ready, s_turned, taps_of_u, h0_ready) = S.values()
        s_x = [sem(f"s_x{j}") for j in range(KEPT)]
        s_w = [sem(f"s_w{r}") for r in range(RING)]
        s_wp = [sem(f"s_wp{r}") for r in range(RING)]
        s_xs = [sem(f"s_xs{j}") for j in range(2)]
        s_y = [sem(f"s_y{j}") for j in range(2)]
        s_gather = [sem(f"s_gather{t}") for t in range(TILES)]

        block = ctx.enter_context(nc.Block())

        small = [(w_sb, w_in), (id_sb[:, :], ident), (g1_sb[:, :], g1), (b1_sb[:, :], b1), (rows_sb[:, :, :], rows),
                 (chan[0][:, :], chan_m), (chan[1][:, :], chan_t), (hp[0][:, :, :], hp_m), (hp[1][:, :, :], hp_t),
                 (step_sb[:, :], steps)]
        later = [(pos_sb, pos), (cls_sb[:, :], cls), (wlin[0], wlin_m), (wlin[1], wlin_t),
                 (wout[0], wout_m), (wout[1], wout_t), (gate[0][:, :], gate_m),
                 (gate[1][:, :], gate_t), (gateb_sb[:, :], gate_b), (tab[:, :], tables), (upper_sb[:, :], upper)]
        NSMALL = 16 * len(small)
        NFRONT = 16 * len(later)
        N_DMAS = (3, 3, 1)
        POOL_HIGH = (NX - LATE) * CHUNKS + RING

        def half(hb):
            return slice(64 * hb, 64 * hb + 64)

        def weights(e, q):
            at = e * SLOT + (q * 3 * I if q < 2 else W2_AT)
            n = 3 if q < 2 else 2
            w = I if q < 2 else IC * D
            return w16[:, at:at + n * w].rearrange("p (a n) -> p a n", a=n)

        def loaded(eng, c):
            by = s_wp if c >= POOL_HIGH else s_w
            first = POOL_HIGH if c >= POOL_HIGH else 0
            eng.wait_ge(by[c % RING], 16 * sum(N_DMAS[k % 3] for k in range(first, c + 1) if k % RING == c % RING))

        def at_least(eng, s, value):
            if not isinstance(value, int) or value > 0:
                eng.wait_ge(s, value)

        def load_chunk(eng, c):
            e, q = divmod(c, CHUNKS)
            r = c % RING
            by = s_wp if c >= POOL_HIGH else s_w
            if c >= RING:
                eng.wait_ge(lo_split, c - RING + 1)
            src = (w1, w3)[q] if q < 2 else w2
            if q < 2:
                eng.dma_start(stage[:, r, 0:I], src[e, 0:P, :]).then_inc(by[r], 16)
                for hb in range(HB):
                    eng.dma_start(stage[half(hb), r, I:2 * I], src[e, P:D, :]).then_inc(by[r], 16)
            else:
                eng.dma_start(stage[:, r, 0:IC * D].rearrange("p (c n) -> p c n", c=IC),
                             src[e].rearrange("(c p) n -> p c n", p=P)).then_inc(by[r], 16)

        @block.sync
        def _(sp):
            for dst, src in small:
                sp.dma_start(dst, src).then_inc(s_small, 16)

            def patches(t):
                k = t % KEPT
                if t >= KEPT:
                    sp.wait_ge(stats_done, t - KEPT + 1)
                    sp.wait_ge(emb_ready, t - KEPT + 1)
                sp.dma_start(xt[:, k, :], xtok[t]).then_inc(s_x[k], 16)
                sp.dma_start(xf[:, k, :, :], xfeat[t]).then_inc(s_x[k], 16)

            for t in range(KEPT):
                patches(t)
            for dst, src in later:
                sp.dma_start(dst, src).then_inc(s_front, 16)
            for c in range(RING):
                load_chunk(sp, c)
            for t in range(KEPT, TILES):
                patches(t)
            for c in range(RING, POOL_HIGH):
                load_chunk(sp, c)
                if c == RING:
                    sp.wait_ge(zero_set, 1)
                    sp.dma_start(x_rows[TILES * P:, :].rearrange("(s p) n -> p s n", p=P),
                                 zeros[:, :].rearrange("p (a n) -> p a n", a=1).to_broadcast([P, ROUTED, ROW])).then_inc(zero_out, 16)
            for hb in range(HB):
                sp.wait_ge(xlo_ready, 2 * (hb + 1))
                ts = slice(hb * TH, (hb + 1) * TH)
                sp.dma_start(x_rows[hb * TH * P:(hb + 1) * TH * P, :].rearrange("(t p) n -> p t n", p=P), xr[:, ts, :]).then_inc(s_rows, 16)
            sp.wait_ge(s_rows, 16 * HB)

            def load_x(s, par):
                sp.dma_start(xs[:, par, :], x_rows[bass.ts(s, P), :]).then_inc(s_xs[par], 16)

            def store_y(s, par):
                sp.wait_ge(y_copied, s + 1)
                sp.dma_start(y_rows[bass.ts(s, P), :], ybuf[:, par, :]).then_inc(s_y[par], 16)

            def pair(p, first=False, last=False):
                for par in range(2):
                    s = 2 * p + par
                    if not last:
                        sp.wait_ge(x_turned, s + 1)
                        load_x(s + 2, par)
                    if not (first and par == 0):
                        store_y(s - 1, 1 - par)

            load_x(0, 0)
            load_x(1, 1)
            pair(0, first=True)
            with sp.Fori(1, SHARED_PAIRS - 1) as p:
                pair(p)
            sp.wait_ge(s_scatter, 16 * TILES * TOPK)
            with sp.Fori(SHARED_PAIRS - 1, PAIRS - 1) as p:
                pair(p)
            pair(PAIRS - 1, last=True)
            store_y(NT - 1, 1)
            sp.dma_start(shared_y[:, :, :], y_rows[0:TILES * P, :].rearrange("(t p) n -> p t n", p=P)).then_inc(s_shared, 16)
            for hb in range(HB):
                for j in range(TH):
                    n = min(LT, L - j * LT)
                    sp.wait_ge(summed, hb * TH + j + 1)
                    sp.dma_start(out[hb * BH:(hb + 1) * BH, j * LT:j * LT + n, :].rearrange("b l e -> l b e"),
                                 h_tok[0:n * BH, hb * TH + j, :]).then_inc(s_out, 16)
            sp.wait_ge(s_out, 16 * TILES)
            sp.wait_ge(s_y[0], 16 * PAIRS)
            sp.wait_ge(s_y[1], 16 * PAIRS)

        @block.gpsimd
        def _(pool):
            chain = [0]

            def link(ins):
                chain[0] += 1
                ins.then_inc(pool_c, 1)
                pool.wait_ge(pool_c, chain[0])
            pool.memset(ones[:, :], 1.0).then_inc(ones_set, 1)
            pool.memset(zeros[:, :], 0.0).then_inc(zero_set, 1)
            pool.wait_ge(s_front, NFRONT)
            pool.tensor_copy(id16[:, :], id_sb[:, :]).then_inc(id16_set, 1)
            pool.wait_ge(id16_set, 1)
            link(pool.tensor_tensor(cls_sb[:, :], cls_sb[:, :], pos_sb[0:BH, 0, :], ALU.add))
            pool.tensor_tensor(pos_sb[:, :, :], pos_sb[:, :, :],
                               rows_sb[:, 2:3, :].to_broadcast([P, TH, D]), ALU.add).then_inc(pos_ready, 1)
            pool.wait_ge(pos_ready, 1)
            pool.tensor_tensor(wout[0][:, 0:P], wout[0][:, 0:P], id_sb[:, :], ALU.add).then_inc(wout_ready, 1)
            pool.wait_ge(wout_ready, 1)
            pool.tensor_tensor(wout[1][0:64, P:D], wout[1][0:64, P:D], id_sb[0:64, 0:64], ALU.add).then_inc(wout_ready, 1)
            pool.wait_ge(wout_ready, 2)
            pool.tensor_tensor(wout[1][64:P, P:D], wout[1][64:P, P:D], id_sb[64:P, 64:P], ALU.add).then_inc(wout_ready, 1)
            pool.wait_ge(wout_ready, 3)

            def split_low(c, high_too=False):
                e, q = divmod(c, CHUNKS)
                r = c % RING
                w = weights(e, q)
                n = I if q < 2 else IC * D
                loaded(pool, c)
                if high_too:
                    pool.tensor_copy(w[:, 0, :], stage[:, r, 0:n]).then_inc(pool_c, 1)
                    chain[0] += 1
                    if q < 2:
                        pool.tensor_copy(w[:, 2, :], stage[:, r, I:2 * I]).then_inc(pool_c, 1)
                        chain[0] += 1
                    pool.wait_ge(pool_c, chain[0])
                else:
                    pool.wait_ge(hi_split, c + 1)
                if q < 2:
                    link(pool.tensor_tensor(w[64:P, 2, :], stage[64:P, r, I:2 * I], w[64:P, 2, :], ALU.subtract))
                pool.tensor_tensor(w[:, 1, :], stage[:, r, 0:n], w[:, 0, :], ALU.subtract).then_inc(lo_split, 1)
                pool.wait_ge(lo_split, c + 1)

            for c in range(POOL_HIGH):
                split_low(c)
                if c + RING >= POOL_HIGH:
                    load_chunk(pool, c + RING)
                if c == POOL_HIGH - 1:
                    pool.wait_ge(slots_ready, 1)
                    pool.wait_ge(zero_out, 16)
                    for t in range(TILES):
                        n = min(LT, L - (t % TH) * LT) * BH
                        for k in range(TOPK):
                            pool.indirect_dma_start(x_rows, bass.IndirectOffsetOnAxis(slot_i[0:n, k, t:t + 1], 0),
                                                    xr[0:n, t, :], None).then_inc(s_scatter, 16)
                    pool.wait_ge(s_scatter, 16 * TILES * TOPK)
            for c in range(POOL_HIGH, NX * CHUNKS):
                split_low(c, high_too=True)
                if c + RING < NX * CHUNKS:
                    load_chunk(pool, c + RING)
            pool.wait_ge(s_y[0], 16 * PAIRS)
            pool.wait_ge(s_y[1], 16 * PAIRS)
            for t in range(TILES):
                n = min(LT, L - (t % TH) * LT) * BH
                for k in range(TOPK):
                    pool.indirect_dma_start(gathered[0:n, t, k, :], None, y_rows,
                                            bass.IndirectOffsetOnAxis(slot_i[0:n, k, t:t + 1], 0)).then_inc(s_gather[t], 16)

        @block.scalar
        def _(act):
            chain = [0]

            def link(ins):
                chain[0] += 1
                ins.then_inc(act_c, 1)
                act.wait_ge(act_c, chain[0])
            act.wait_ge(s_small, NSMALL)
            for k in range(2):
                act.activation(win[k][:, :], step_sb[:, :], ACT.Exp, scale=chan[k][:, C_ALPHA:C_ALPHA + 1]).then_inc(win_exp, 1)

            done = [0]

            def split_high(n):
                for c in range(done[0], done[0] + n):
                    e, q = divmod(c, CHUNKS)
                    r = c % RING
                    loaded(act, c)
                    w = weights(e, q)
                    if q < 2:
                        act.activation(w[:, 0:3:2, :], stage[:, r, :].rearrange("p (a n) -> p a n", a=2), ACT.Copy).then_inc(hi_split, 1)
                    else:
                        act.activation(w[:, 0, :], stage[:, r, 0:IC * D], ACT.Copy).then_inc(hi_split, 1)
                done[0] += n

            act.wait_ge(hw_ready, 2)
            for k in range(2):
                act.activation(habs[k][:, :, :], hp[k][:, :, :], ACT.Abs).then_inc(habs_ready, 1)

            def sqrt(n):
                for hb in range(HB):
                    act.wait_ge(var_ready, 2 * n + hb + 1)
                    act.activation(std[:, hb * TH:(hb + 1) * TH], std[:, hb * TH:(hb + 1) * TH], ACT.Sqrt).then_inc(std_ready, 1)

            def diagonals(i):
                act.wait_ge(h0_ready, 2)
                for m in range(2):
                    for j in range(PE_LAGS[i]):
                        tap = hp[m][:, i, j:j + 1] if j else h0[m][:, i:i + 1]
                        act.activation(diag[i][:, m, j, :], id_sb[:, :], ACT.Copy, scale=tap).then_inc(diag_ready, 1)

            sqrt(0)
            diagonals(0)
            sqrt(1)
            act.wait_ge(emb_ready, TILES)
            act.wait_ge(cols_ready, 1)
            diagonals(1)
            sqrt(2)
            split_high(1)

            def copy_uT(n, m, t):
                for hb in range(HB):
                    act.wait_ge(uT_ready, 2 * n + hb + 1)
                    act.activation(m[:, hb, :], ps_flat[:, hb * 2048:hb * 2048 + COLS], ACT.Copy).then_inc(u_ready, 1)
                    act.activation(t[half(hb), 0, :], ps_flat[half(hb), hb * 2048 + 1024:hb * 2048 + 1024 + COLS], ACT.Copy).then_inc(u_ready, 1)

            copy_uT(0, u[0], u[1])
            k = 0
            for n, (part, dst) in enumerate(((0, x[0]), (1, x[1]), (2, v))):
                if n:
                    split_high(1)
                    act.wait_ge(taps_done, 2 * n)
                for m in range(2):
                    for hb in range(HB if m == 0 else 1):
                        for s in range(2):
                            act.wait_ge(zps_ready, k + 1)
                            act.activation(z[m][:, hb, s * SPLIT:(s + 1) * SPLIT], ps[:, 5 + k % 3, 0:SPLIT], ACT.Identity,
                                           bias=chan[m][:, C_BLIN + part:C_BLIN + part + 1]).then_inc(z_copied, 1)
                            k += 1
                act.wait_ge(z_copied, k)
                for m in range(2):
                    act.activation(dst[m][:, :, :], z[m][:, :, :], ACT.Identity, bias=chan[m][:, C_CONVB + part:C_CONVB + part + 1],
                                   scale=chan[m][:, C_TAP + 3 * part + 2:C_TAP + 3 * part + 3]).then_inc(tap2_ready, 1)
            def exps(i):
                act.wait_ge(nmx_ready, i + 1)
                for t in range(TILES):
                    act.activation(x_tok[i][:, t, :], ps_tok[:, t // TH, t % TH, 0:D], ACT.Exp, bias=mx[:, i, t:t + 1],
                                   accum_out=sums[:, i, t:t + 1]).then_inc(exp_done, 1)

            def scale_rows(i):
                act.wait_ge(rec_ready, i + 1)
                for t in range(TILES):
                    act.activation(x_tok[i][:, t, :], x_tok[i][:, t, :], ACT.Copy, scale=sums[:, i, t:t + 1]).then_inc(soft_ready, 1)

            def copy_back(i):
                for r in range(4):
                    act.wait_ge(s_turned, 4 * i + r + 1)
                    to = soft[i][0][:, r, :] if r < 2 else soft[i][1][half(r - 2), 0, :]
                    src = ps_flat[:, 3072:3072 + COLS] if r < 2 else ps_flat[half(r - 2), 3072:3072 + COLS]
                    act.activation(to, src, ACT.Copy).then_inc(s_copied, 1)

            exps(0)
            split_high(2)
            scale_rows(0)
            exps(1)
            copy_back(0)
            split_high(1)
            scale_rows(1)
            copy_back(1)
            split_high((NX - LATE) * CHUNKS - done[0] - 1)
            split_high(1)
            sqrt(3)
            for hb in range(HB):
                ts = slice(hb * TH, (hb + 1) * TH)
                act.wait_ge(utok_ready, TILES + (hb + 1) * TH)
                act.activation(xr[:, ts, 0:P], u_tok[:, ts, 0:P], ACT.Copy).then_inc(xhi_ready, 1)
                for r in range(2):
                    ins = act.activation(xr[:, ts, P + r * DT:P + (r + 1) * DT], u_tok[:, ts, P:D], ACT.Copy)
                    if r:
                        ins.then_inc(xhi_ready, 1)
            copy_uT(1, u[0], u[1])
            act.wait_ge(g1s, 1)
            act.activation(gs[:, 1, :], gs[:, 0, :], ACT.Exp, scale=-1.0).then_inc(gexp, 1)
            act.wait_ge(g2s, 1)
            act.activation(gs[:, 3, :], gs[:, 2, :], ACT.Ln).then_inc(gln, 1)
            act.wait_ge(g3s, 1)
            act.activation(gs[:, 5, :], gs[:, 4, :], ACT.Sqrt).then_inc(gsq, 1)
            split_high(POOL_HIGH - done[0])

            def silu(s, hh):
                k = 2 * s + hh
                act.wait_ge(up_done, k + 1)
                at_least(act, h_ready, k - 1)
                act.activation(sg[:, hh, :], ps[:, hh, 0:HI], ACT.Silu).then_inc(silu_done, 1)

            def high(s, hh):
                k = 2 * s + hh
                act.wait_ge(h_ready, k + 1)
                at_least(act, h_turned, k - 1)
                act.activation(hhl[:, hh, 0, :], hid[:, hh, :], ACT.Copy).then_inc(hi_done, 1)

            def copy_x(s, par):
                act.wait_ge(x_turned, s + 1)
                at_least(act, up_done, 2 * s - 2)
                act.activation(xT[:, par, :, :].rearrange("p a n -> p (a n)"), psum16(6, ROW), ACT.Copy).then_inc(x_copied, 1)

            def copy_hb(s, par):
                act.wait_ge(h_turned, 2 * s + 2)
                at_least(act, down_done, s - 1)
                act.activation(hT[:, par, 1, :], psum16(5, 2 * HI), ACT.Copy).then_inc(hb_copied, 1)

            def pair(p, first=False, last=False):
                for par in range(2):
                    s = 2 * p + par
                    silu(s, 0)
                    if not (first and par == 0):
                        copy_hb(s - 1, 1 - par)
                    high(s, 0)
                    silu(s, 1)
                    if not (last and par == 1):
                        copy_x(s + 1, 1 - par)
                    high(s, 1)

            copy_x(0, 0)
            pair(0, first=True)
            with act.Fori(1, PAIRS - 1) as p:
                pair(p)
            pair(PAIRS - 1, last=True)
            copy_hb(NT - 1, 1)

        @block.vector
        def _(dve):
            chain = [0]

            def link(ins):
                chain[0] += 1
                ins.then_inc(dve_c, 1)
                dve.wait_ge(dve_c, chain[0])

            vr = [0]

            def norm_stats(src, hb, width, n):
                t0 = hb * TH
                for t in range(t0, t0 + TH):
                    if n == 0:
                        dve.wait_ge(s_x[t % KEPT], 32 * (t // KEPT + 1))
                    for k in range(width // 384 if width > 384 else 1):
                        w = min(width, 384)
                        link(dve.bn_stats(stat[:, t, k, :], src[:, t % KEPT if n == 0 else t, k * w:(k + 1) * w]))
                    nk = 2 if width > 384 else 1
                    ins = dve.bn_aggr(mv[:, t, :], stat[:, t, 0:nk, :])
                    if n == 0:
                        ins.then_inc(stats_done, 1)
                        dve.wait_ge(stats_done, t + 1)
                    else:
                        link(ins)
                dve.tensor_scalar(std[:, t0:t0 + TH], mv[:, t0:t0 + TH, 1], EPS, None, ALU.add).then_inc(var_ready, 1)

            def norm_scale(hb, n):
                t0 = hb * TH
                dve.wait_ge(std_ready, 2 * n + hb + 1)
                link(dve.reciprocal(rstd[:, t0:t0 + TH], std[:, t0:t0 + TH]))

            dve.wait_ge(s_small, NSMALL)
            dve.wait_ge(ones_set, 1)
            for c in range(FC):
                dve.tensor_scalar(wg_sb[:, c, :], w_sb[:, c, :], g1_sb[:, c:c + 1], None, ALU.mult).then_inc(wg_ready, 1)
                dve.tensor_scalar(b1_wide[:, c, :], ones[:, :], b1_sb[:, c:c + 1], None, ALU.mult).then_inc(wg_ready, 1)
            dve.wait_ge(win_exp, 2)
            for k in range(2):
                link(dve.tensor_scalar(win[k][:, :], win[k][:, :], chan[k][:, C_WINB:C_WINB + 1], None, ALU.add))
                dve.tensor_tensor(hp[k][:, :, :], hp[k][:, :, :], win[k][:, :].rearrange("p (a n) -> p a n", a=1).to_broadcast([P, ORDER, L]),
                                  ALU.mult).then_inc(hw_ready, 1)
            norm_stats(xt, 0, PD, 0)
            dve.wait_ge(hsum_ready, 1)
            link(dve.reciprocal(hrec[:, :, :], ps[:, 7, 0:ORDER * L].rearrange("p (o l) -> p o l", o=ORDER)))
            for k in range(2):
                link(dve.tensor_tensor(hp[k][:, :, :], hp[k][:, :, :], hrec[:, :, :], ALU.mult))
                dve.tensor_tensor(h0[k][:, :], hp[k][:, :, 0], chan[k][:, C_BMAT:C_BMAT + ORDER], ALU.add).then_inc(h0_ready, 1)
            dve.wait_ge(cols_ready, 1)
            link(dve.tensor_copy(colsum[:, :], ps[:, 6, 0:D]))
            link(dve.tensor_tensor(shift[:, :], ps[:, 6, 256:256 + D], rows_sb[:, 0, :], ALU.add))
            norm_stats(xt, 1, PD, 0)
            for hb in range(HB):
                t0 = hb * TH
                ts = slice(t0, t0 + TH)
                norm_scale(hb, 0)
                link(dve.scalar_tensor_tensor(out=nmr[:, ts], in0=mv[:, ts, 0], scalar=-1.0, in1=rstd[:, ts], op0=ALU.mult, op1=ALU.mult))
                dve.wait_ge(emb_ready, t0 + TH)
                for t in range(t0, t0 + TH):
                    dve.tensor_scalar(u_tok[:, t, :], ps_tok[:, t // TH, t % TH, 0:D], rstd[:, t:t + 1], None, ALU.mult).then_inc(emb_read, 1)
                dve.wait_ge(emb_read, t0 + TH)
                for t in range(t0, t0 + TH):
                    link(dve.scalar_tensor_tensor(out=u_tok[:, t, :], in0=colsum[:, :], scalar=nmr[:, t:t + 1], in1=u_tok[:, t, :], op0=ALU.mult, op1=ALU.add))
                sh = shift[:, :].rearrange("p (a n) -> p a n", a=1).to_broadcast([P, TH, D])
                link(dve.tensor_tensor(u_tok[:, ts, :], u_tok[:, ts, :], sh, ALU.add))
                norm_stats(u_tok, hb, D, 1)
            for hb in range(HB):
                t0 = hb * TH
                ts = slice(t0, t0 + TH)
                norm_scale(hb, 1)
                for t in range(t0, t0 + TH):
                    link(dve.tensor_scalar(h_tok[:, t, :], u_tok[:, t, :], mv[:, t, 0:1], rstd[:, t:t + 1], ALU.subtract, ALU.mult))
                link(dve.tensor_tensor(h_tok[:, ts, :], h_tok[:, ts, :], rows_sb[:, 1:2, :].to_broadcast([P, TH, D]), ALU.mult))
                dve.wait_ge(pos_ready, 1)
                link(dve.tensor_tensor(h_tok[:, ts, :], h_tok[:, ts, :], pos_sb[:, :, :], ALU.add))
                link(dve.tensor_copy(h_tok[0:BH, t0, :], cls_sb[:, :]))
                norm_stats(h_tok, hb, D, 2)
            for hb in range(HB):
                t0 = hb * TH
                ts = slice(t0, t0 + TH)
                norm_scale(hb, 2)
                for t in range(t0, t0 + TH):
                    dve.tensor_scalar(u_tok[:, t, :], h_tok[:, t, :], mv[:, t, 0:1], rstd[:, t:t + 1], ALU.subtract, ALU.mult).then_inc(utok_ready, 1)
                dve.wait_ge(utok_ready, t0 + TH)
                link(dve.tensor_tensor(h_tok[:, ts, :], h_tok[:, ts, :], rows_sb[:, 3:4, :].to_broadcast([P, TH, D]), ALU.add))
            def row_max(i):
                dve.wait_ge(xT_ready, i + 1)
                link(dve.tensor_reduce(mx[:, i, :].rearrange("p (h t) -> p h t", h=HB), ps_tok[:, :, 0:TH, 0:D], AX.X, ALU.max))
                dve.tensor_scalar(mx[:, i, :], mx[:, i, :], -1.0, None, ALU.mult).then_inc(nmx_ready, 1)

            def row_scale(i):
                dve.wait_ge(exp_done, TILES * (i + 1))
                dve.reciprocal(sums[:, i, :], sums[:, i, :]).then_inc(rec_ready, 1)

            for n, (part, dst) in enumerate(((0, x[0]), (1, x[1]), (2, v))):
                dve.wait_ge(tap2_ready, 2 * n + 2)
                for m in range(2):
                    for back in (1, 2):
                        o = back * BH
                        tap = chan[m][:, C_TAP + 3 * part + 2 - back:C_TAP + 3 * part + 3 - back]
                        ins = dve.scalar_tensor_tensor(out=dst[m][:, :, o:], in0=z[m][:, :, 0:COLS - o], scalar=tap,
                                                       in1=dst[m][:, :, o:], op0=ALU.mult, op1=ALU.add)
                        if back == 1:
                            link(ins)
                        else:
                            ins.then_inc(taps_done, 1)
                dve.wait_ge(taps_done, 2 * n + 2)
                if part == 1:
                    row_max(0)
                if part == 2:
                    for m in range(2):
                        dve.tensor_tensor(v[m][:, :, :], v[m][:, :, :], u[m][:, :, :], ALU.add).then_inc(v_base, 1)
            dve.wait_ge(v_base, 2)
            between = {PE_LAGS[0] + 4: lambda: row_scale(0), PE_LAGS[0] + 8: lambda: row_max(1),
                       PE_LAGS[0] + 13: lambda: row_scale(1)}
            for i in range(ORDER):
                first = PE_LAGS[i]
                for m in range(2):
                    link(dve.memset(y[m][:, :, 0:first * BH], 0.0))
                for j in range(first, L):
                    o = j * BH
                    if i == 0 and j in between:
                        between[j]()
                    for m in range(2):
                        if j == first:
                            link(dve.tensor_scalar(y[m][:, :, o:REAL], v[m][:, :, 0:REAL - o], hp[m][:, i, j:j + 1], None, ALU.mult))
                        else:
                            link(dve.scalar_tensor_tensor(out=y[m][:, :, o:REAL], in0=v[m][:, :, 0:REAL - o], scalar=hp[m][:, i, j:j + 1],
                                                          in1=y[m][:, :, o:REAL], op0=ALU.mult, op1=ALU.add))
                dve.wait_ge(conv_ready, i + 1)
                dve.wait_ge(s_copied, 4 * (i + 1))
                for m in range(2):
                    n = HB if m == 0 else 1
                    both = y[m][:, :, 0:REAL].rearrange("p h (b c) -> p h b c", b=2)
                    link(dve.tensor_tensor(both, both, ps[:, 4 * m:4 * m + 2 * n, 0:CB].rearrange("p (h b) c -> p h b c", h=n), ALU.add))
                    link(dve.tensor_tensor(y[m][:, :, 0:REAL], y[m][:, :, 0:REAL], soft[i][m][:, :, 0:REAL], ALU.mult))
                    dve.tensor_tensor(v[m][:, :, 0:REAL], v[m][:, :, 0:REAL], y[m][:, :, 0:REAL], ALU.add).then_inc(v_ready, 1)
                dve.wait_ge(v_ready, 2 * (i + 1))
            for hb in range(HB):
                t0 = hb * TH
                ts = slice(t0, t0 + TH)
                dve.wait_ge(o_ready, (hb + 1) * TH)
                link(dve.tensor_tensor(h_tok[:, ts, :], h_tok[:, ts, :], ps_tok[:, hb, 0:TH, 0:D], ALU.add))
                norm_stats(h_tok, hb, D, 3)
            for hb in range(HB):
                t0 = hb * TH
                norm_scale(hb, 3)
                for t in range(t0, t0 + TH):
                    dve.tensor_scalar(u_tok[:, t, :], h_tok[:, t, :], mv[:, t, 0:1], rstd[:, t:t + 1], ALU.subtract, ALU.mult).then_inc(utok_ready, 1)
            for hb in range(HB):
                ts = slice(hb * TH, (hb + 1) * TH)
                dve.wait_ge(xhi_ready, 2 * (hb + 1))
                dve.tensor_tensor(xr[:, ts, 2 * P:3 * P], u_tok[:, ts, 0:P], xr[:, ts, 0:P], ALU.subtract).then_inc(xlo_ready, 1)
                for r in range(2):
                    ins = dve.tensor_tensor(xr[:, ts, 3 * P + r * DT:3 * P + (r + 1) * DT], u_tok[:, ts, P:D],
                                            xr[:, ts, P:P + DT], ALU.subtract)
                    if r:
                        ins.then_inc(xlo_ready, 1)
            dve.wait_ge(gate_ps, 1)
            G = gs
            link(dve.tensor_copy(G[:, 6, :].rearrange("p (h n) -> p h n", h=HB), ps[:, 6:8, 0:TH * E]))
            link(dve.tensor_scalar(G[:, 7, :], G[:, 6, :], -1.0, None, ALU.mult))
            dve.tensor_tensor(G[:, 0, :], G[:, 6, :], G[:, 7, :], ALU.max).then_inc(g1s, 1)
            dve.wait_ge(gexp, 1)
            dve.tensor_scalar(G[:, 2, :], G[:, 1, :], 1.0, None, ALU.add).then_inc(g2s, 1)
            dve.wait_ge(g2s, 1)
            link(dve.tensor_scalar(G[:, 8, :], G[:, 2, :], 1.0, None, ALU.subtract))
            link(dve.tensor_scalar(G[:, 9, :], G[:, 8, :], 0.0, None, ALU.is_equal))
            link(dve.tensor_tensor(G[:, 8, :], G[:, 8, :], G[:, 9, :], ALU.add))
            link(dve.reciprocal(G[:, 8, :], G[:, 8, :]))
            link(dve.tensor_tensor(G[:, 8, :], G[:, 8, :], G[:, 1, :], ALU.mult))
            dve.wait_ge(gln, 1)
            link(dve.tensor_tensor(G[:, 3, :], G[:, 3, :], G[:, 9, :], ALU.max))
            link(dve.tensor_tensor(G[:, 3, :], G[:, 3, :], G[:, 8, :], ALU.mult))
            dve.scalar_tensor_tensor(out=G[:, 4, :], in0=G[:, 6, :], scalar=0.0, in1=G[:, 3, :], op0=ALU.max, op1=ALU.add).then_inc(g3s, 1)
            dve.wait_ge(gsq, 1)
            
            def v3(k):
                return G[:, k, :].rearrange("p (t e) -> p t e", e=E)

            def over(k):
                return gr[:, k, :].rearrange("p (t a) -> p t a", a=1).to_broadcast([P, TILES, E])
            link(dve.tensor_tensor(v3(6), v3(5), gateb_sb[:, :].rearrange("p (a e) -> p a e", a=1).to_broadcast([P, TILES, E]), ALU.add))
            for k in range(2):
                link(dve.tensor_reduce(gr[:, k, :], v3(6), AX.X, ALU.max))
                link(dve.tensor_tensor(v3(7), v3(6), over(k), ALU.is_equal))
                link(dve.tensor_tensor(G[:, 7, :], G[:, 7, :], tab[:, T_DOWN:T_DOWN + TILES * E], ALU.mult))
                link(dve.tensor_reduce(gr[:, 2, :], v3(7), AX.X, ALU.max))
                link(dve.tensor_tensor(v3(10 + k), v3(7), over(2), ALU.is_equal))
                if k == 0:
                    link(dve.scalar_tensor_tensor(out=G[:, 6, :], in0=G[:, 10, :], scalar=-1e30, in1=G[:, 6, :], op0=ALU.mult, op1=ALU.add))
            real = tab[:, T_REAL:T_REAL + TILES].rearrange("p (t a) -> p t a", a=1).to_broadcast([P, TILES, E])
            for k in range(TOPK):
                link(dve.tensor_tensor(v3(10 + k), v3(10 + k), real, ALU.mult))
            dve.tensor_tensor(G[:, 12, :], G[:, 10, :], G[:, 11, :], ALU.add).then_inc(m_ready, 1)
            for k in range(TOPK):
                link(dve.tensor_tensor(G[:, 8, :], G[:, 10 + k, :], G[:, 5, :], ALU.mult))
                link(dve.tensor_reduce(wk[:, k, :], v3(8), AX.X, ALU.add))
            link(dve.tensor_tensor(gr[:, 2, :], wk[:, 0, :], wk[:, 1, :], ALU.add))
            link(dve.tensor_scalar(gr[:, 2, :], gr[:, 2, :], 1e-6, None, ALU.max))
            link(dve.reciprocal(gr[:, 3, :], gr[:, 2, :]))
            for k in range(TOPK):
                link(dve.tensor_tensor(wk[:, k, :], wk[:, k, :], gr[:, 3, :], ALU.mult))
            dve.wait_ge(pre_ready, 1)
            link(dve.memset(run[:, 0, :], 0.0))
            for t in range(TILES):
                link(dve.tensor_tensor(run[:, t + 1, :], run[:, t, :], ps[:, 7, P + t * E:P + (t + 1) * E], ALU.add))
            sc = scratch[:, 0:E * TILES].rearrange("p (e k) -> p e k", e=E)
            link(dve.tensor_tensor(sc, run[:, TILES, :].rearrange("p (e a) -> p e a", a=1).to_broadcast([P, E, TILES]),
                                   tab[:, T_FULL:T_FULL + TILES].rearrange("p (a k) -> p a k", a=1).to_broadcast([P, E, TILES]), ALU.is_gt))
            link(dve.tensor_reduce(tiles_of[:, :], sc, AX.X, ALU.add))
            link(dve.memset(first_tile[:, 0:1], 0.0))
            for e in range(E):
                link(dve.tensor_tensor(first_tile[:, e + 1:e + 2], first_tile[:, e:e + 1], tiles_of[:, e:e + 1], ALU.add))
            link(dve.tensor_tensor(G[:, 8, :], ps[:, 7, 0:TILES * E], run[:, 0:TILES, :].rearrange("p t e -> p (t e)"), ALU.add))
            link(dve.tensor_scalar(gr[:, 0, 0:E], first_tile[:, 0:E], float(P), float(TILES * P), ALU.mult, ALU.add))
            link(dve.tensor_tensor(v3(8), v3(8), gr[:, 0, 0:E].rearrange("p (a e) -> p a e", a=1).to_broadcast([P, TILES, E]), ALU.add))
            for k in range(TOPK):
                link(dve.tensor_tensor(G[:, 9, :], G[:, 8, :], G[:, 10 + k, :], ALU.mult))
                link(dve.tensor_reduce(slot_f[:, k, :], v3(9), AX.X, ALU.add))
            dve.tensor_copy(slot_i[:, :, :], slot_f[:, :, :]).then_inc(slots_ready, 1)
            sc = scratch[0:1, :].rearrange("p (s e) -> p s e", s=ROUTED)
            link(dve.tensor_tensor(sc, tab[0:1, T_TILE:T_TILE + ROUTED].rearrange("p (s a) -> p s a", a=1).to_broadcast([1, ROUTED, E]),
                                   first_tile[0:1, 1:E + 1].rearrange("p (a e) -> p a e", a=1).to_broadcast([1, ROUTED, E]), ALU.is_ge))
            link(dve.memset(place_f[:, 0:TILES], 0.0))
            link(dve.tensor_reduce(place_f[:, TILES:], sc, AX.X, ALU.add))
            link(dve.tensor_scalar(place_f[:, TILES:], place_f[:, TILES:], float(E - 1), 1.0, ALU.min, ALU.add))
            link(dve.tensor_scalar(place_f[:, :], place_f[:, :], float(SLOT), None, ALU.mult))
            dve.tensor_copy(place_i[:, :], place_f[:, :]).then_inc(place_ready, 1)

            def clip(s, hh):
                dve.wait_ge(up_done, 2 * s + hh + 1)
                dve.tensor_scalar(uc[:, hh, :], ps[:, 2 + hh, 0:HI], LIMIT, -LIMIT, ALU.min, ALU.max).then_inc(clip_done, 1)

            def hidden(s, hh):
                k = 2 * s + hh
                dve.wait_ge(silu_done, k + 1)
                dve.wait_ge(clip_done, k + 1)
                at_least(dve, lo_done, k - 1)
                dve.scalar_tensor_tensor(out=hid[:, hh, :], in0=sg[:, hh, :], scalar=SILU_LIMIT, in1=uc[:, hh, :],
                                         op0=ALU.min, op1=ALU.mult).then_inc(h_ready, 1)

            def low(s, hh):
                k = 2 * s + hh
                dve.wait_ge(hi_done, k + 1)
                dve.tensor_tensor(hhl[:, hh, 1, :], hid[:, hh, :], hhl[:, hh, 0, :], ALU.subtract).then_inc(lo_done, 1)

            def copy_ha(s, par):
                dve.wait_ge(h_turned, 2 * s + 1)
                at_least(dve, down_done, s - 1)
                dve.tensor_copy(hT[:, par, 0, :], psum16(4, 2 * HI)).then_inc(ha_copied, 1)

            def copy_y(s, par, n_stored):
                dve.wait_ge(down_done, s + 1)
                at_least(dve, s_y[par], n_stored)
                dve.tensor_copy(ybuf[:, par, :], ps[:, 7, 0:D]).then_inc(y_copied, 1)

            def pair(p, first=False):
                for par in range(2):
                    s = 2 * p + par
                    clip(s, 0)
                    hidden(s, 0)
                    low(s, 0)
                    clip(s, 1)
                    hidden(s, 1)
                    low(s, 1)
                    if par:
                        copy_y(s - 1, 0, 16 * p)
                    elif not first:
                        copy_y(s - 1, 1, 16 * (p - 1))
                    copy_ha(s, par)

            pair(0, first=True)
            pair(1)
            with dve.Fori(2, PAIRS) as p:
                pair(p)
            copy_y(NT - 1, 1, 16 * (PAIRS - 1))
            dve.wait_ge(s_shared, 16)
            link(dve.tensor_tensor(h_tok[:, :, :], h_tok[:, :, :], shared_y[:, :, :], ALU.add))
            for t in range(TILES):
                n = min(LT, L - (t % TH) * LT) * BH
                dve.wait_ge(s_gather[t], 16 * TOPK)
                for k in range(TOPK):
                    ins = dve.scalar_tensor_tensor(out=h_tok[0:n, t, :], in0=gathered[0:n, t, k, :], scalar=wk[0:n, k, t:t + 1],
                                                   in1=h_tok[0:n, t, :], op0=ALU.mult, op1=ALU.add)
                    if k == TOPK - 1:
                        ins.then_inc(summed, 1)
                    else:
                        link(ins)

        @block.tensor
        def _(pe):
            def mm(o, lhsT, rhs, first, last):
                return pe.matmul(o, lhsT, rhs, start=first, stop=last, skip_group_check=True)

            pe.wait_ge(s_small, NSMALL)
            pe.wait_ge(ones_set, 1)
            pe.wait_ge(wg_ready, 2 * FC)
            for c in range(FC):
                mm(ps[:, 6, 0:D], ones[:, :], wg_sb[:, c, :], c == 0, c == FC - 1)
            for c in range(FC):
                last = mm(ps[:, 6, 256:256 + D], b1_wide[:, c, :], w_sb[:, c, :], c == 0, c == FC - 1)
            last.then_inc(cols_ready, 1)
            pe.wait_ge(habs_ready, 2)
            mm(ps[:, 7, 0:ORDER * L], ones[:, :], habs[0][:, :, :].rearrange("p o l -> p (o l)"), True, False)
            mm(ps[:, 7, 0:ORDER * L], ones[0:64, :], habs[1][0:64, :, :].rearrange("p o l -> p (o l)"), False, True).then_inc(hsum_ready, 1)
            for t in range(TILES):
                pe.wait_ge(s_x[t % KEPT], 32 * (t // KEPT + 1))
                for c in range(FC):
                    last = mm(ps_tok[:, t // TH, t % TH, 0:D], xf[:, t % KEPT, c, :], wg_sb[:, c, :], c == 0, c == FC - 1)
                last.then_inc(emb_ready, 1)
            pe.wait_ge(emb_ready, TILES)

            def transpose_tail(hb, o, t, src=u_tok):
                if hb == 0:
                    return pe.transpose(ps_flat[0:DT, o:o + P], src[:, t, P:D], id_sb[:, :])
                return pe.transpose(ps_flat[:, o:o + P], src[:, t, D - P:D], id_sb[:, :])

            def transpose_u(n):
                for hb in range(HB):
                    for j in range(TH):
                        t = hb * TH + j
                        pe.wait_ge(utok_ready, n * TILES + t + 1)
                        o = hb * 2048 + j * P
                        pe.transpose(ps_flat[:, o:o + P], u_tok[:, t, 0:P], id_sb[:, :])
                        last = transpose_tail(hb, o + 1024, t)
                    last.then_inc(uT_ready, 1)

            pe.wait_ge(s_front, NFRONT)
            pe.wait_ge(emb_read, TILES)
            transpose_u(0)
            pe.wait_ge(u_ready, 4)
            k = 0

            def project(part):
                nonlocal k
                c0 = part * D
                for m in range(2):
                    for hb in range(HB if m == 0 else 1):
                        for s in range(2):
                            if k >= 3:
                                pe.wait_ge(z_copied, k - 2)
                            cs = slice(s * SPLIT, (s + 1) * SPLIT)
                            if m == 0:
                                o = ps[:, 5 + k % 3, 0:SPLIT]
                                mm(o, wlin[0][:, c0:c0 + P], u[0][:, hb, cs], True, False)
                                last = mm(o, wlin[1][half(hb), c0:c0 + P], u[1][half(hb), 0, cs], False, True)
                            else:
                                for h in range(HB):
                                    o = ps[half(h), 5 + k % 3, 0:SPLIT]
                                    mm(o, wlin[0][:, c0 + P:c0 + D], u[0][:, h, cs], True, False)
                                    last = mm(o, wlin[1][half(h), c0 + P:c0 + D], u[1][half(h), 0, cs], False, True)
                            last.then_inc(zps_ready, 1)
                            k += 1

            def to_tokens(i):
                for t in range(TILES):
                    hb, j = divmod(t, TH)
                    cs = slice(j * P, (j + 1) * P)
                    pe.transpose(ps_tok[:, hb, j, 0:P], x[i][0][:, hb, cs], id_sb[:, :])
                    last = pe.transpose(ps_tok[:, hb, j, P:D], x[i][1][half(hb), 0, cs], id_sb[half(hb), half(hb)])
                last.then_inc(xT_ready, 1)

            def to_channels(i):
                pe.wait_ge(soft_ready, (i + 1) * TILES)
                for r in range(4):
                    at_least(pe, s_copied, 4 * i + r)
                    for j in range(TH):
                        t = (r % 2) * TH + j
                        o = 3072 + j * P
                        if r < 2:
                            last = pe.transpose(ps_flat[:, o:o + P], x_tok[i][:, t, 0:P], id_sb[:, :])
                        else:
                            last = transpose_tail(r - 2, o, t, x_tok[i])
                    last.then_inc(s_turned, 1)

            def long_conv(i):
                pe.wait_ge(diag_ready, 2 * sum(PE_LAGS[0:i + 1]))
                for a in range(3):
                    m, hb = divmod(a, HB)
                    for j in range(PE_LAGS[i]):
                        for b in range(2):
                            lo, hi = max(j * BH, b * CB), (b + 1) * CB
                            last = mm(ps[:, 2 * a + b, lo - b * CB:CB], diag[i][:, m, j, :], v[m][:, hb, lo - j * BH:hi - j * BH],
                                      j == 0, j == PE_LAGS[i] - 1)
                last.then_inc(conv_ready, 1)

            project(0)
            project(1)
            project(2)
            pe.wait_ge(taps_done, 2)
            pe.wait_ge(z_copied, k)
            to_tokens(0)
            pe.wait_ge(taps_done, 4)
            pe.wait_ge(exp_done, TILES)
            to_tokens(1)
            to_channels(0)
            pe.wait_ge(exp_done, 2 * TILES)
            pe.wait_ge(v_base, 2)
            long_conv(0)
            to_channels(1)
            pe.wait_ge(v_ready, 2)
            long_conv(1)
            pe.wait_ge(v_ready, 4)
            pe.wait_ge(wout_ready, 3)
            for t in range(TILES):
                hb, j = divmod(t, TH)
                cs = slice(j * P, (j + 1) * P)
                mm(ps_tok[:, t // TH, t % TH, 0:D], v[0][:, hb, cs], wout[0][:, :], True, False)
                mm(ps_tok[:, t // TH, t % TH, 0:D], v[1][half(hb), 0, cs], wout[1][half(hb), :], False, True).then_inc(o_ready, 1)
            pe.wait_ge(var_ready, 8)
            transpose_u(1)
            pe.wait_ge(u_ready, 8)
            for t in range(TILES):
                hb, j = divmod(t, TH)
                cs = slice(j * P, (j + 1) * P)
                mm(ps[:, 6 + hb, j * E:(j + 1) * E], u[0][:, hb, cs], gate[0][:, :], True, False)
                last = mm(ps[:, 6 + hb, j * E:(j + 1) * E], u[1][half(hb), 0, cs], gate[1][half(hb), :], False, True)
            last.then_inc(gate_ps, 1)
            pe.wait_ge(m_ready, 1)
            n8 = TILES * E
            mm(ps[:, 7, 0:n8], upper_sb[:, :], gs[:, 12, :], True, True)
            mm(ps[:, 7, P:P + n8], ones[:, :], gs[:, 12, :], True, True).then_inc(pre_ready, 1)

            def turn_x(s, par, n):
                pe.wait_ge(s_xs[par], n)
                at_least(pe, x_copied, s)
                for a in range(4):
                    last = pe.transpose(psum16(6, ROW)[:, a * P:(a + 1) * P], xs[:, par, a * P:(a + 1) * P], id16[:, :])
                last.then_inc(x_turned, 1)

            def up(s, par, hh, place):
                pe.wait_ge(x_copied, s + 1)
                at_least(pe, h_ready, 2 * s + hh - 1)
                for n in range(2):
                    for i, (a, b) in enumerate(((0, 0), (0, 1), (2, 0), (1, 2), (3, 2))):
                        at = place + (n * 3 * I + b * I + hh * HI)
                        last = mm(ps[:, 2 * n + hh, 0:HI], xT[:, par, a, :], w16[:, bass.ds(at, HI)], i == 0, i == 4)
                last.then_inc(up_done, 1)

            def turn_h(s, hh):
                k = 2 * s + hh
                pe.wait_ge(lo_done, k + 1)
                at_least(pe, (ha_copied, hb_copied)[hh], s)
                for a in range(2 * IC // 2):
                    last = pe.transpose(psum16(4 + hh, 2 * HI)[:, a * P:(a + 1) * P],
                                        hhl[:, hh, :, :].rearrange("p a n -> p (a n)")[:, a * P:(a + 1) * P], id16[:, :])
                last.then_inc(h_turned, 1)

            def down(s, par, place):
                pe.wait_ge(ha_copied, s + 1)
                pe.wait_ge(hb_copied, s + 1)
                at_least(pe, y_copied, s)
                for c in range(IC):
                    hh, i = divmod(c, IC // 2)
                    for a, b in ((0, 0), (0, 1), (1, 0)):
                        at = place + (W2_AT + b * IC * D + c * D)
                        last = mm(ps[:, 7, 0:D], hT[:, par, hh, a * HI + i * P:a * HI + (i + 1) * P], w16[:, bass.ds(at, D)],
                                  c == 0 and a == b == 0, c == IC - 1 and a == 1)
                last.then_inc(down_done, 1)

            def place_of(s):
                return pe.value_load(place_i[0:1, bass.ds(s, 1)], min_val=0, max_val=E * SLOT)

            def pair(p, first=False, last=False):
                for par in range(2):
                    s = 2 * p + par
                    here = place_of(s)
                    up(s, par, 0, here)
                    if not (first and par == 0):
                        turn_h(s - 1, 1)
                    up(s, par, 1, here)
                    before = None if first and par == 0 else place_of(s - 1)
                    if not (last and par == 1):
                        turn_x(s + 1, 1 - par, 16 * (p + 1 + par))
                    if before is not None:
                        down(s - 1, 1 - par, before)
                    turn_h(s, 0)

            pe.wait_ge(id16_set, 1)
            pe.wait_ge(place_ready, 1)
            pe.wait_ge(lo_split, CHUNKS)
            turn_x(0, 0, 16)
            pair(0, first=True)
            with pe.Fori(1, SHARED_PAIRS) as p:
                pair(p)
            pe.wait_ge(lo_split, NX * CHUNKS)
            with pe.Fori(SHARED_PAIRS, PAIRS - 1) as p:
                pair(p)
            pair(PAIRS - 1, last=True)
            turn_h(NT - 1, 1)
            down(NT - 1, 1, place_of(NT - 1))


def kernel(**inputs):
    import numpy as np
    import concourse.bacc as bacc
    from concourse.bass_utils import run_bass_kernel_spmd

    a = {k: np.ascontiguousarray(v) for k, v in inputs.items()}
    f32 = np.float32

    def tiles(m):
        n = m.shape[2]
        padded = np.zeros((HB, LP, BH, n), f32)
        padded[:, :m.shape[1]] = m.reshape(HB, BH, m.shape[1], n).transpose(0, 2, 1, 3)
        return padded.reshape(TILES, P, n)

    def wide(row):
        return np.ascontiguousarray(np.broadcast_to(row, (P,) + row.shape))

    def split(m):
        return np.ascontiguousarray(m[:P]), np.concatenate([m[P:], m[P:]])

    patches = a["x"].reshape(B, 3, 6, 16, 6, 16).transpose(0, 2, 4, 3, 5, 1).reshape(B, 36, PD)
    patches = np.concatenate([np.zeros((B, 1, PD), f32), patches], axis=1)
    xtok = tiles(patches)
    pos = np.zeros((LP, D), f32)
    pos[:L] = a["L0_tok_pos_embed"][0]
    chan = np.concatenate([a["L0_attn_b_lin"].reshape(3, D).T,
                           a["L0_attn_conv_w"].reshape(3, D, 3).transpose(1, 0, 2).reshape(D, 9),
                           a["L0_attn_conv_b"].reshape(3, D).T, a["L0_attn_alphas"].reshape(D, 1),
                           a["L0_attn_win_b"].reshape(D, 1), a["L0_attn_Bmat"].reshape(ORDER, D).T], axis=1)
    ins = {
        "xtok": xtok,
        "xfeat": xtok.reshape(TILES, P, FC, P).transpose(0, 3, 2, 1),
        "pos": pos.reshape(TH, LT, 1, D).repeat(BH, 2).reshape(TH, P, D).transpose(1, 0, 2),
        "ident": np.eye(P, dtype=f32),
        "steps": wide(np.linspace(0.0, 1.0, 512, dtype=f32)[:L]),
        "w_in": a["L0_tok_W"].reshape(FC, P, D).transpose(1, 0, 2),
        "g1": a["L0_tok_ln1_g"].reshape(FC, P).T,
        "b1": a["L0_tok_ln1_b"].reshape(FC, P).T,
        "rows": wide(np.stack([a["L0_tok_b"], a["L0_tok_ln2_g"], a["L0_tok_ln2_b"], a["L0_attn_b_out"]])),
        "cls": np.broadcast_to(a["L0_tok_cls_token"], (BH, D)),
    }
    ins["wlin_m"], ins["wlin_t"] = split(a["L0_attn_W_lin"].T)
    ins["chan_m"], ins["chan_t"] = split(chan)
    ins["hp_m"], ins["hp_t"] = split(a["L0_attn_h_param"].transpose(1, 0, 2)[:, :, :L])
    ins["wout_m"], ins["wout_t"] = split(a["L0_attn_W_out"].T)
    ins["gate_m"], ins["gate_t"] = split(a["L0_ffn_gate_w"])
    ins["gate_b"] = wide(a["L0_ffn_gate_bias"])
    table = np.zeros((P, NTAB), f32)
    where = np.arange(P)[:, None] // BH + LT * (np.arange(TILES)[None, :] % TH)
    table[:, T_REAL:T_REAL + TILES] = where < L
    table[:, T_DOWN:T_FULL] = np.tile(np.arange(E, 0, -1), TILES)
    table[:, T_FULL:T_TILE] = P * np.arange(TILES)
    table[:, T_TILE:] = np.arange(ROUTED)
    ins["tables"] = table
    ins["upper"] = np.triu(np.ones((P, P), f32), 1)
    for n in ("w1", "w3", "w2"):
        ins[n] = np.concatenate([a["L0_ffn_" + n + "s"][None], a["L0_ffn_" + n]])

    nc = bacc.Bacc("TRN2", target_bir_lowering=False, num_devices=1)
    arrays, args = {}, []
    for name, m in ins.items():
        arrays["in_" + name] = np.ascontiguousarray(m)
        args.append(nc.dram_tensor("in_" + name, m.shape, F32, kind="ExternalInput").ap())
    args.append(nc.dram_tensor("out_0", (B, L, D), F32, kind="ExternalOutput").ap())
    build(nc, *args)
    r = run_bass_kernel_spmd(nc, [arrays], core_ids=[0])
    return r.results[0]["out_0"]
```

```python
from contextlib import ExitStack

import concourse.bass as bass
from concourse import mybir

ALU = mybir.AluOpType
ACT = mybir.ActivationFunctionType
F32 = mybir.dt.float32
F16 = mybir.dt.float16
I32 = mybir.dt.int32
AX = mybir.AxisListType

P = 128
B = 32
HB = 2
BH = B // HB
L = 37
LT = P // BH
TH = -(-L // LT)
LP = TH * LT
TILES = HB * TH
COLS = LP * BH
REAL = L * BH
PD = 768
FC = PD // P
D = 192
DT = D - P
ORDER = 2
PE_LAGS = (6, 11)
PARTS = ((1, 0), (0, 0), (0, 1))
CB = REAL // 2
E = 8
I = 768
IC = I // P
EPS = 1e-5
LIMIT = 10.0
SILU_LIMIT = 9.999546021312975
SPLIT = COLS // 2
TOPK = 2
NX = E + 1
HI = I // 2
ROUTED = (TOPK * B * L + E * (P - 1)) // P
NT = TILES + ROUTED
GROUP = 8
GROUPS = (ROUTED - 2) // GROUP
assert TILES % 2 == 0 and ROUTED == GROUP * GROUPS + 2
ROW = 4 * P
XW = ROW // 2 + 1
SLOT = 6 * I + 2 * IC * D
W2_AT = 6 * I
CHUNKS = 3
CHUNK = 2 * I
RING = 3
KEPT = 7
TURNED = 4
C_BLIN, C_TAP, C_CONVB, C_ALPHA, C_WINB, C_BMAT = 0, 3, 12, 15, 16, 17
NCH = C_BMAT + ORDER
T_REAL, T_DOWN = 0, TILES
T_FULL, T_TILE = T_DOWN + TILES * E, T_DOWN + TILES * E + TILES
T_ID = T_TILE + ROUTED
T_PAD = T_ID + TILES
NTAB = T_PAD + ROUTED


def build(nc, xtok, pos, ident, steps, w_in, g1, b1, rows, cls, wlin_m, wlin_t, chan_m, chan_t,
          hp_m, hp_t, wout_m, wout_t, gate_m, gate_t, gate_b, tables, upper, w1, w3, w2, out):
    with ExitStack() as ctx:
        def sb(name, shape, dt=F32):
            return ctx.enter_context(nc.sbuf_tensor(name, shape, dt))

        def sem(name):
            return ctx.enter_context(nc.semaphore(name))

        ps = ctx.enter_context(nc.psum_tensor("ps", [P, 8, 512], F32))
        ps_tok = ps[:, 0:6, :].rearrange("p (a b) (h n) -> p a (b h) n", a=HB, h=2)
        ps_flat = ps[:, :, :].rearrange("p b n -> p (b n)")

        def psum16(bank, n):
            return ps[:, bank, 0:n // 2].bitcast(F16)

        def cut(tensor, dt=F32):
            at = [0]

            def take(*shape, dtype=F32):
                n = 1
                for k in shape:
                    n *= k
                words = n // 2 if dtype == F16 else n
                view = tensor[:, at[0]:at[0] + words]
                at[0] += words
                assert at[0] <= tensor.shape[1], (at[0], tensor.shape)
                if dtype == F16:
                    view = view.bitcast(F16)
                if len(shape) == 1:
                    return view
                names = "abcd"[:len(shape)]
                return view.rearrange(f"p ({' '.join(names)}) -> p {' '.join(names)}", **dict(zip(names, shape)))
            return take

        id_sb = sb("id_sb", [P, P])
        id16 = sb("id16", [P, P], F16)
        ones = sb("ones", [P, P])
        y_at = sb("y_at", [P, 4, 1], I32)
        g1_sb = sb("g1_sb", [P, FC])
        b1_sb = sb("b1_sb", [P, FC])
        rows_sb = sb("rows_sb", [P, 4, D])
        cls_sb = sb("cls_sb", [BH, D])
        chan = [sb("chan_m_sb", [P, NCH]), sb("chan_t_sb", [P, NCH])]
        hp = [sb("hp_m_sb", [P, ORDER, L]), sb("hp_t_sb", [P, ORDER, L])]
        habs = [sb("habs_m", [P, ORDER, L]), sb("habs_t", [P, ORDER, L])]
        win = [sb("win_m", [P, L]), sb("win_t", [P, L])]
        hrec = sb("hrec", [P, ORDER, L])
        h0 = [sb("h0_m", [P, ORDER]), sb("h0_t", [P, ORDER])]
        step_sb = sb("step_sb", [P, L])
        gate = [sb("gate_m_sb", [P, E]), sb("gate_t_sb", [P, HB * E])]
        gateb_sb = sb("gateb_sb", [P, E])
        stat = sb("stat", [P, TILES, 2, 6])
        mv = sb("mv", [P, TILES, 2])
        std = sb("std", [P, TILES])
        rstd = sb("rstd", [P, TILES])
        h_tok = sb("h_tok", [P, TILES, D])
        u_tok = sb("u_tok", [P, TILES, D])
        mx = sb("mx", [P, ORDER, TILES])
        sums = sb("sums", [P, ORDER, TILES])
        gs = sb("gs", [P, 14, TILES * E])
        gr = sb("gr", [P, 4, TILES])
        tab = sb("tab", [P, NTAB])
        upper_sb = sb("upper_sb", [P, P])
        run = sb("run", [P, TILES + 1, E])
        tiles_of = sb("tiles_of", [P, E])
        first_tile = sb("first_tile", [P, E + 1])
        counts = sb("counts", [P, 2, TILES * E])
        scratch = sb("scratch", [P, ROUTED * E])
        wk = sb("wk", [P, TOPK, TILES])
        slot_f = sb("slot_f", [P, TOPK, TILES])
        slot_i = sb("slot_i", [P, TOPK, TILES], I32)
        place_f = sb("place_f", [1, ROUTED])
        place_i = sb("place_i", [1, ROUTED], I32)
        slots = sb("slots", [P, NX * SLOT // 2])
        w16 = slots[:, :].bitcast(F16)
        stage = sb("stage", [P, RING, CHUNK])
        LATE = 3
        take = cut(slots[:, (NX - LATE) * SLOT // 2:])
        u = [take(HB, COLS), take(1, COLS)]
        v = [take(HB, COLS), take(1, COLS)]
        z = [take(HB, COLS), take(1, COLS)]
        x = [[take(HB, COLS), take(1, COLS)] for _ in range(ORDER)]
        y = z
        x_at = (NX - LATE) * SLOT // 2 + 9 * COLS
        x_tok = [slots[:, x_at + 3 * COLS * i:x_at + 3 * COLS * (i + 1)].rearrange("p (t n) -> p t n", t=TILES) for i in range(ORDER)]
        u_flat = u_tok[:, :, :].rearrange("p t n -> p (t n)")
        soft = [[u_flat[:, 0:HB * COLS].rearrange("p (h n) -> p h n", h=HB),
                 u_flat[:, HB * COLS:].rearrange("p (h n) -> p h n", h=1)], x[0]]
        take = cut(slots[:, (NX - LATE) * SLOT // 2 + 3 * COLS:])
        xt = take(KEPT, PD)
        xf = take(TURNED, FC, P)
        BLANK_IN = NX - LATE - 2
        blank = slots[:, BLANK_IN * SLOT // 2:BLANK_IN * SLOT // 2 + ROUTED * XW].rearrange("p (s n) -> p s n", s=ROUTED)
        assert ROUTED * XW <= SLOT
        gathered = slots[:, 0:TILES * TOPK * D].rearrange("p (t k n) -> p t k n", t=TILES, k=TOPK)
        front = sb("front", [P, 8832])
        take = cut(front)
        w_sb = take(FC, D)
        wg_sb = take(FC, D)
        b1_wide = take(FC, P)
        POS_AT = FC * (2 * D + P)
        pos_sb = take(TH, D)
        assert COLS <= TH * D
        shift = take(D)
        wlin = [take(3 * D), take(3 * D)]
        wout = [take(D), take(D)]
        diag = [take(2, PE_LAGS[0], P)]
        diag.append(cut(front)(2, PE_LAGS[1], P))
        zs = [z, [take(HB, COLS), front[:, POS_AT:POS_AT + COLS].rearrange("p (a n) -> p a n", a=1)]]
        take = cut(front)
        xr_words = take(TILES, XW)
        xs_words = take(2, XW)
        rows16 = front[:, 0:(TILES + 2) * XW].bitcast(F16).rearrange("p (t n) -> p t n", n=2 * XW)
        xr = rows16[:, 0:TILES, :]
        xs = rows16[:, TILES:, :]
        xT = take(2, 4, P, dtype=F16)
        sg = take(2, HI)
        uc = take(2, HI)
        hid = take(2, HI)
        hhl = take(2, 2, HI, dtype=F16)
        hT = take(2, 2, 2 * HI, dtype=F16)
        ybuf = take(2, D)
        x_rows = nc.dram_tensor("x_rows", [ROUTED * P, XW], F32).ap()
        y_rows = nc.dram_tensor("y_rows", [(TOPK * TILES + ROUTED) * P, D], F32).ap()

        (s_small, s_front, s_out, ones_set, dve_c, act_c, pool_c, wg_ready, win_exp, hw_ready,
         habs_ready, hsum_ready, xf_turned, xf_copied, shift_ps, shift_set, wc_ready, first_added,
         cols_ready, emb_ready, emb_read, var_ready, std_ready, utok_ready, uT_ready, u_ready, z_ready,
         z_copied, tap2_ready, taps_done, xT_ready, exp_done, sum_recip_ready, soft_ready, s_copied,
         v_ready, wout_ready, o_ready, gate_ps, gate_exp, gate_log, gate_root, gate_abs, gate_exp1,
         gate_softplus, pos_ready, nmx_ready, blank_set, at_copied, rows_cleared, stats_done, xhi_ready,
         xlo_ready, chosen_ready, counts_ready, counts_copied, slots_ready, place_ready, s_scatter,
         hi_split, lo_split, x_turned, x_copied, up_done, silu_done, clip_done, h_ready, hi_done,
         lo_done, h_turned, ha_copied, hb_copied, down_done, y_copied, summed, id16_set, diag_ready,
         v_base, conv_ready, s_turned, h0_ready) = (sem(name) for name in """
            s_small s_front s_out ones_set dve_c act_c pool_c wg_ready win_exp hw_ready habs_ready
            hsum_ready xf_turned xf_copied shift_ps shift_set wc_ready first_added cols_ready
            emb_ready emb_read var_ready std_ready utok_ready uT_ready u_ready z_ready z_copied
            tap2_ready taps_done xT_ready exp_done sum_recip_ready soft_ready s_copied v_ready
            wout_ready o_ready gate_ps gate_exp gate_log gate_root gate_abs gate_exp1 gate_softplus
            pos_ready nmx_ready blank_set at_copied rows_cleared stats_done xhi_ready xlo_ready
            chosen_ready counts_ready counts_copied slots_ready place_ready s_scatter hi_split
            lo_split x_turned x_copied up_done silu_done clip_done h_ready hi_done lo_done h_turned
            ha_copied hb_copied down_done y_copied summed id16_set diag_ready v_base conv_ready
            s_turned h0_ready""".split())
        s_x = [sem(f"s_x{j}") for j in range(KEPT)]
        s_w = [sem(f"s_w{r}") for r in range(RING)]
        s_xs = [sem(f"s_xs{j}") for j in range(2)]
        s_y = [sem(f"s_y{j}") for j in range(2)]
        s_gather = [sem(f"s_gather{t}") for t in range(TILES)]

        block = ctx.enter_context(nc.Block())

        small = [(w_sb, w_in), (id_sb[:, :], ident), (g1_sb[:, :], g1), (b1_sb[:, :], b1), (rows_sb[:, :, :], rows),
                 (chan[0][:, :], chan_m), (chan[1][:, :], chan_t), (hp[0][:, :, :], hp_m), (hp[1][:, :, :], hp_t),
                 (step_sb[:, :], steps)]
        later = [(pos_sb, pos), (cls_sb[:, :], cls), (wlin[0], wlin_m), (wlin[1], wlin_t),
                 (wout[0], wout_m), (wout[1], wout_t), (gate[0][:, :], gate_m),
                 (gate[1][:, :], gate_t), (gateb_sb[:, :], gate_b), (tab[:, :], tables), (upper_sb[:, :], upper)]
        NSMALL = 16 * len(small)
        NFRONT = 16 * len(later)
        N_DMAS = (3, 3, 1)
        EARLY = (NX - LATE) * CHUNKS

        def half(hb):
            return slice(64 * hb, 64 * hb + 64)

        def weights(e, q):
            at = e * SLOT + (q * 3 * I if q < 2 else W2_AT)
            n = 3 if q < 2 else 2
            w = I if q < 2 else IC * D
            return w16[:, at:at + n * w].rearrange("p (a n) -> p a n", a=n)

        def loaded(eng, c):
            eng.wait_ge(s_w[c % RING], 16 * sum(N_DMAS[k % 3] for k in range(c + 1) if k % RING == c % RING))

        def at_least(eng, s, value):
            if not isinstance(value, int) or value > 0:
                eng.wait_ge(s, value)

        def load_chunk(eng, c):
            e, q = divmod(c, CHUNKS)
            r = c % RING
            if c >= RING:
                eng.wait_ge(lo_split, c - RING + 1)
            src = (w1, w3)[q] if q < 2 else w2
            if q < 2:
                eng.dma_start(stage[:, r, 0:I], src[e, 0:P, :]).then_inc(s_w[r], 16)
                for hb in range(HB):
                    eng.dma_start(stage[half(hb), r, I:2 * I], src[e, P:D, :]).then_inc(s_w[r], 16)
            else:
                eng.dma_start(stage[:, r, 0:IC * D].rearrange("p (c n) -> p c n", c=IC),
                             src[e].rearrange("(c p) n -> p c n", p=P)).then_inc(s_w[r], 16)

        @block.sync
        def _(sp):
            for dst, src in small:
                sp.dma_start(dst, src).then_inc(s_small, 16)

            for t in range(TILES):
                if t >= KEPT:
                    sp.wait_ge(stats_done, t - KEPT + 1)
                    sp.wait_ge(xf_turned, 2 * (t - KEPT + 1))
                sp.dma_start(xt[:, t % KEPT, :], xtok[t]).then_inc(s_x[t % KEPT], 16)
            for dst, src in later:
                sp.dma_start(dst, src).then_inc(s_front, 16)
            for c in range(RING):
                load_chunk(sp, c)
            for c in range(RING, NX * CHUNKS):
                load_chunk(sp, c)
                if c == RING:
                    sp.wait_ge(blank_set, 2)
                    sp.dma_start(x_rows.rearrange("(s p) n -> p s n", p=P), blank).then_inc(rows_cleared, 16)
            sp.wait_ge(s_scatter, 16 * TILES * TOPK)

            def load_x(s, par):
                sp.dma_start(xs_words[:, par, :], x_rows[bass.ts(s - TILES, P), :]).then_inc(s_xs[par], 16)

            def tiles(s0, n):
                for i in range(n):
                    sp.wait_ge(at_copied, s0 + i - TILES + 1)
                    load_x(s0 + i + 2, i % 2)

            load_x(TILES, 0)
            load_x(TILES + 1, 1)
            tiles(TILES, GROUP)
            with sp.Fori(1, GROUPS) as q:
                tiles(q * GROUP + TILES, GROUP)
            for par in range(2):
                sp.wait_ge(s_y[par], 8 * ROUTED)
            for t in range(TILES):
                n = min(LT, L - (t % TH) * LT) * BH
                sp.dma_start(gathered[0:n, t, :, :],
                             y_rows[0:TOPK * TILES * P, :].rearrange("(k t p) n -> p t k n", k=TOPK, t=TILES)[0:n, t, :, :]).then_inc(s_gather[t], 16)
            for hb in range(HB):
                for j in range(TH):
                    n = min(LT, L - j * LT)
                    sp.wait_ge(summed, hb * TH + j + 1)
                    sp.dma_start(out[hb * BH:(hb + 1) * BH, j * LT:j * LT + n, :].rearrange("b l e -> l b e"),
                                 h_tok[0:n * BH, hb * TH + j, :]).then_inc(s_out, 16)
            sp.wait_ge(s_out, 16 * TILES)

        @block.gpsimd
        def _(pool):
            chain = [0]

            def link(ins):
                chain[0] += 1
                ins.then_inc(pool_c, 1)
                pool.wait_ge(pool_c, chain[0])
            pool.memset(ones[:, :], 1.0).then_inc(ones_set, 1)
            pool.memset(blank, 0.0).then_inc(blank_set, 1)
            pool.wait_ge(s_front, NFRONT)
            pool.tensor_copy(id16[:, :], id_sb[:, :]).then_inc(id16_set, 1)
            pool.wait_ge(id16_set, 1)
            pool.wait_ge(blank_set, 1)
            pool.tensor_copy(blank[:, :, XW - 1], tab[:, T_PAD:T_PAD + ROUTED]).then_inc(blank_set, 1)
            pool.wait_ge(blank_set, 2)
            link(pool.tensor_tensor(cls_sb[:, :], cls_sb[:, :], pos_sb[0:BH, 0, :], ALU.add))
            pool.tensor_tensor(pos_sb[:, :, :], pos_sb[:, :, :],
                               rows_sb[:, 2:3, :].to_broadcast([P, TH, D]), ALU.add).then_inc(pos_ready, 1)
            pool.wait_ge(pos_ready, 1)
            pool.tensor_tensor(wout[0][:, 0:P], wout[0][:, 0:P], id_sb[:, :], ALU.add).then_inc(wout_ready, 1)
            pool.wait_ge(wout_ready, 1)
            pool.tensor_tensor(wout[1][0:64, P:D], wout[1][0:64, P:D], id_sb[0:64, 0:64], ALU.add).then_inc(wout_ready, 1)
            pool.wait_ge(wout_ready, 2)
            pool.tensor_tensor(wout[1][64:P, P:D], wout[1][64:P, P:D], id_sb[64:P, 64:P], ALU.add).then_inc(wout_ready, 1)
            pool.wait_ge(wout_ready, 3)

            def split_low(c):
                e, q = divmod(c, CHUNKS)
                r = c % RING
                w = weights(e, q)
                n = I if q < 2 else IC * D
                loaded(pool, c)
                pool.wait_ge(hi_split, c + 1)
                if q < 2:
                    link(pool.tensor_tensor(w[64:P, 2, :], stage[64:P, r, I:2 * I], w[64:P, 2, :], ALU.subtract))
                pool.tensor_tensor(w[:, 1, :], stage[:, r, 0:n], w[:, 0, :], ALU.subtract).then_inc(lo_split, 1)
                pool.wait_ge(lo_split, c + 1)

            def scatter(k, t):
                n = min(LT, L - (t % TH) * LT) * BH
                pool.indirect_dma_start(x_rows, bass.IndirectOffsetOnAxis(slot_i[0:n, k, t:t + 1], 0),
                                        xr_words[0:n, t, :], None).then_inc(s_scatter, 16)

            for c in range(NX * CHUNKS - 3):
                split_low(c)
            pool.wait_ge(xlo_ready, 2 * HB)
            link(pool.tensor_copy(xr_words[:, :, XW - 1], tab[:, T_ID:T_ID + TILES]))
            pool.wait_ge(slots_ready, 1)
            pool.wait_ge(rows_cleared, 16)
            for t in range(TILES):
                scatter(0, t)
            pool.wait_ge(s_scatter, 16 * TILES)
            link(pool.tensor_scalar(xr_words[:, :, XW - 1], xr_words[:, :, XW - 1], float(TILES * P), None, ALU.add))
            for c in range(NX * CHUNKS - 3, NX * CHUNKS):
                split_low(c)
            for t in range(TILES):
                scatter(1, t)
            pool.wait_ge(s_scatter, 16 * TILES * TOPK)

            def take_at(i):
                pool.wait_ge(s_xs[i % 2], 16 * (i // 2 + 1))
                pool.wait_ge(x_turned, TILES + i + 1)
                if i >= 3:
                    pool.wait_ge(s_y[(i - 3) % 2], 16 * ((i - 3) // 2 + 1))
                pool.tensor_copy(y_at[:, i % 4, :], xs_words[:, i % 2, XW - 1:XW]).then_inc(at_copied, 1)

            def store_y(i):
                pool.wait_ge(y_copied, TILES + i + 1)
                pool.wait_ge(at_copied, i + 1)
                pool.indirect_dma_start(y_rows, bass.IndirectOffsetOnAxis(y_at[:, i % 4, :], 0), ybuf[:, i % 2, :], None).then_inc(s_y[i % 2], 16)

            take_at(0)
            take_at(1)
            for i in range(ROUTED):
                if i + 2 < ROUTED:
                    take_at(i + 2)
                store_y(i)

        @block.scalar
        def _(act):
            chain = [0]

            def link(ins):
                chain[0] += 1
                ins.then_inc(act_c, 1)
                act.wait_ge(act_c, chain[0])
            act.wait_ge(s_small, NSMALL)
            for k in range(2):
                act.activation(win[k][:, :], step_sb[:, :], ACT.Exp, scale=chan[k][:, C_ALPHA:C_ALPHA + 1]).then_inc(win_exp, 1)

            done = [0]

            def split_high(n):
                for c in range(done[0], done[0] + n):
                    e, q = divmod(c, CHUNKS)
                    r = c % RING
                    loaded(act, c)
                    if c == BLANK_IN * CHUNKS:
                        act.wait_ge(rows_cleared, 16)
                    w = weights(e, q)
                    if q < 2:
                        act.activation(w[:, 0:3:2, :], stage[:, r, :].rearrange("p (a n) -> p a n", a=2), ACT.Copy).then_inc(hi_split, 1)
                    else:
                        act.activation(w[:, 0, :], stage[:, r, 0:IC * D], ACT.Copy).then_inc(hi_split, 1)
                done[0] += n

            act.wait_ge(hw_ready, 2)
            for k in range(2):
                act.activation(habs[k][:, :, :], hp[k][:, :, :], ACT.Abs).then_inc(habs_ready, 1)

            def sqrt(n, halves=range(HB)):
                for hb in halves:
                    act.wait_ge(var_ready, 2 * n + hb + 1)
                    act.activation(std[:, hb * TH:(hb + 1) * TH], std[:, hb * TH:(hb + 1) * TH], ACT.Sqrt).then_inc(std_ready, 1)

            for t in range(TILES):
                for h in range(2):
                    act.wait_ge(xf_turned, 2 * t + h + 1)
                    at_least(act, emb_ready, t - TURNED + 1)
                    act.activation(xf[:, t % TURNED, h * FC // 2:(h + 1) * FC // 2, :].rearrange("p c n -> p (c n)"),
                                   ps[:, 6 + h, 0:PD // 2], ACT.Copy).then_inc(xf_copied, 1)
                if t == TH + 1:
                    sqrt(0, range(1))

            def diagonals(i):
                act.wait_ge(h0_ready, 2)
                for m in range(2):
                    for j in range(PE_LAGS[i]):
                        tap = hp[m][:, i, j:j + 1] if j else h0[m][:, i:i + 1]
                        act.activation(diag[i][:, m, j, :], id_sb[:, :], ACT.Copy, scale=tap).then_inc(diag_ready, 1)

            sqrt(0, range(1, HB))
            diagonals(0)
            sqrt(1)
            act.wait_ge(emb_ready, TILES)
            act.wait_ge(shift_ps, 1)
            diagonals(1)
            sqrt(2)
            split_high(1)

            def copy_uT(n, m, t):
                for hb in range(HB):
                    act.wait_ge(uT_ready, 2 * n + hb + 1)
                    act.activation(m[:, hb, :], ps_flat[:, hb * 2048:hb * 2048 + COLS], ACT.Copy).then_inc(u_ready, 1)
                    act.activation(t[half(hb), 0, :], ps_flat[half(hb), hb * 2048 + 1024:hb * 2048 + 1024 + COLS], ACT.Copy).then_inc(u_ready, 1)

            copy_uT(0, u[0], u[1])
            k = 0
            for n, (part, dst) in enumerate(((0, x[0]), (1, x[1]), (2, v))):
                if n:
                    split_high(1)
                if n == 2:
                    act.wait_ge(taps_done, 2)
                z = zs[n % 2]
                for m in range(2):
                    for hb in range(HB if m == 0 else 1):
                        for s in range(2):
                            act.wait_ge(z_ready, k + 1)
                            act.activation(z[m][:, hb, s * SPLIT:(s + 1) * SPLIT], ps[:, 5 + k % 3, 0:SPLIT], ACT.Identity,
                                           bias=chan[m][:, C_BLIN + part:C_BLIN + part + 1]).then_inc(z_copied, 1)
                            k += 1
                act.wait_ge(z_copied, k)
                for m in range(2):
                    act.activation(dst[m][:, :, :], z[m][:, :, :], ACT.Identity, bias=chan[m][:, C_CONVB + part:C_CONVB + part + 1],
                                   scale=chan[m][:, C_TAP + 3 * part + 2:C_TAP + 3 * part + 3]).then_inc(tap2_ready, 1)
            def exps(i):
                act.wait_ge(nmx_ready, i + 1)
                for t in range(TILES):
                    act.activation(x_tok[i][:, t, :], ps_tok[:, t // TH, t % TH, 0:D], ACT.Exp, bias=mx[:, i, t:t + 1],
                                   accum_out=sums[:, i, t:t + 1]).then_inc(exp_done, 1)

            def scale_rows(i):
                act.wait_ge(sum_recip_ready, i + 1)
                for t in range(TILES):
                    act.activation(x_tok[i][:, t, :], x_tok[i][:, t, :], ACT.Copy, scale=sums[:, i, t:t + 1]).then_inc(soft_ready, 1)

            def copy_back(i):
                for r in range(4):
                    act.wait_ge(s_turned, 4 * i + r + 1)
                    to = soft[i][0][:, r, :] if r < 2 else soft[i][1][half(r - 2), 0, :]
                    src = ps_flat[:, 3072:3072 + COLS] if r < 2 else ps_flat[half(r - 2), 3072:3072 + COLS]
                    act.activation(to, src, ACT.Copy).then_inc(s_copied, 1)

            exps(0)
            scale_rows(0)
            exps(1)
            copy_back(0)
            split_high(3)
            scale_rows(1)
            copy_back(1)
            split_high((NX - LATE) * CHUNKS - done[0] - 1)
            split_high(1)
            sqrt(3)
            for hb in range(HB):
                ts = slice(hb * TH, (hb + 1) * TH)
                act.wait_ge(utok_ready, TILES + (hb + 1) * TH)
                act.activation(xr[:, ts, 0:P], u_tok[:, ts, 0:P], ACT.Copy).then_inc(xhi_ready, 1)
                for r in range(2):
                    ins = act.activation(xr[:, ts, P + r * DT:P + (r + 1) * DT], u_tok[:, ts, P:D], ACT.Copy)
                    if r:
                        ins.then_inc(xhi_ready, 1)
            copy_uT(1, u[0], u[1])
            def silu(s, hh):
                k = 2 * s + hh
                act.wait_ge(up_done, k + 1)
                at_least(act, h_ready, k - 1)
                act.activation(sg[:, hh, :], ps[:, hh, 0:HI], ACT.Silu).then_inc(silu_done, 1)

            def high(s, hh):
                k = 2 * s + hh
                act.wait_ge(h_ready, k + 1)
                at_least(act, h_turned, k - 1)
                act.activation(hhl[:, hh, 0, :], hid[:, hh, :], ACT.Copy).then_inc(hi_done, 1)

            def copy_x(s, par):
                act.wait_ge(x_turned, s + 1)
                at_least(act, up_done, 2 * s - 2)
                act.activation(xT[:, par, :, :].rearrange("p a n -> p (a n)"), psum16(6, ROW), ACT.Copy).then_inc(x_copied, 1)

            def copy_hb(s, par):
                act.wait_ge(h_turned, 2 * s + 2)
                at_least(act, down_done, s - 1)
                act.activation(hT[:, par, 1, :], psum16(5, 2 * HI), ACT.Copy).then_inc(hb_copied, 1)

            def tiles(s0, n, last=False):
                for i in range(n):
                    s, par = s0 + i, i % 2
                    silu(s, 0)
                    copy_hb(s - 1, 1 - par)
                    high(s, 0)
                    silu(s, 1)
                    if not (last and i == n - 1):
                        copy_x(s + 1, 1 - par)
                    high(s, 1)

            copy_x(0, 0)
            act.wait_ge(gate_abs, 1)
            act.activation(gs[:, 1, :], gs[:, 0, :], ACT.Exp, scale=-1.0).then_inc(gate_exp, 1)
            act.wait_ge(gate_exp1, 1)
            act.activation(gs[:, 3, :], gs[:, 2, :], ACT.Ln).then_inc(gate_log, 1)
            act.wait_ge(gate_softplus, 1)
            act.activation(gs[:, 5, :], gs[:, 4, :], ACT.Sqrt).then_inc(gate_root, 1)
            for s in range(TILES):
                silu(s, 0)
                if s > 0:
                    copy_hb(s - 1, 1 - s % 2)
                high(s, 0)
                silu(s, 1)
                copy_x(s + 1, 1 - s % 2)
                high(s, 1)
                if s < 4:
                    split_high(2)
                elif done[0] < NX * CHUNKS:
                    split_high(1)
            with act.Fori(0, GROUPS) as q:
                tiles(q * GROUP + TILES, GROUP)
            tiles(NT - 2, 2, last=True)
            copy_hb(NT - 1, 1)

        @block.vector
        def _(dve):
            chain = [0]

            def put(ins):
                chain[0] += 1
                ins.then_inc(dve_c, 1)
                return chain[0]

            def settle():
                dve.wait_ge(dve_c, chain[0])

            def link(ins):
                chain[0] += 1
                ins.then_inc(dve_c, 1)
                dve.wait_ge(dve_c, chain[0])

            def patch_stats(t):
                dve.wait_ge(s_x[t % KEPT], 16 * (t // KEPT + 1))
                for k in range(2):
                    put(dve.bn_stats(stat[:, t, k, :], xt[:, t % KEPT, k * PD // 2:(k + 1) * PD // 2]))
                settle()
                dve.bn_aggr(mv[:, t, :], stat[:, t, :, :]).then_inc(stats_done, 1)

            def variances(hb):
                ts = slice(hb * TH, (hb + 1) * TH)
                dve.wait_ge(stats_done, (hb + 1) * TH)
                settle()
                dve.tensor_scalar(std[:, ts], mv[:, ts, 1], EPS, None, ALU.add).then_inc(var_ready, 1)

            def norm_stats(src, hb):
                for t in range(hb * TH, (hb + 1) * TH):
                    put(dve.bn_stats(stat[:, t, 0, :], src[:, t, :]))
                settle()
                for t in range(hb * TH, (hb + 1) * TH):
                    put(dve.bn_aggr(mv[:, t, :], stat[:, t, 0:1, :]))
                variances(hb)

            def norm_scale(hb, n):
                t0 = hb * TH
                dve.wait_ge(std_ready, 2 * n + hb + 1)
                link(dve.reciprocal(rstd[:, t0:t0 + TH], std[:, t0:t0 + TH]))

            dve.wait_ge(s_small, NSMALL)
            dve.wait_ge(ones_set, 1)
            for c in range(FC):
                dve.tensor_scalar(wg_sb[:, c, :], w_sb[:, c, :], g1_sb[:, c:c + 1], None, ALU.mult).then_inc(wg_ready, 1)
                dve.tensor_scalar(b1_wide[:, c, :], ones[:, :], b1_sb[:, c:c + 1], None, ALU.mult).then_inc(wg_ready, 1)
            dve.wait_ge(win_exp, 2)
            for k in range(2):
                link(dve.tensor_scalar(win[k][:, :], win[k][:, :], chan[k][:, C_WINB:C_WINB + 1], None, ALU.add))
                dve.tensor_tensor(hp[k][:, :, :], hp[k][:, :, :], win[k][:, :].rearrange("p (a n) -> p a n", a=1).to_broadcast([P, ORDER, L]),
                                  ALU.mult).then_inc(hw_ready, 1)
            patch_stats(0)
            dve.wait_ge(cols_ready, 1)
            dve.scalar_tensor_tensor(out=wg_sb, in0=ps[:, 5, 0:D].rearrange("p (a n) -> p a n", a=1).to_broadcast([P, FC, D]),
                                     scalar=-1.0 / PD, in1=wg_sb, op0=ALU.mult, op1=ALU.add).then_inc(wc_ready, 1)
            for t in range(1, TH):
                patch_stats(t)
            variances(0)
            dve.wait_ge(hsum_ready, 1)
            link(dve.reciprocal(hrec[:, :, :], ps[:, 4, 256:256 + ORDER * L].rearrange("p (o l) -> p o l", o=ORDER)))
            dve.tensor_tensor(shift[:, :], ps[:, 4, 0:D], rows_sb[:, 0, :], ALU.add).then_inc(shift_set, 1)
            dve.wait_ge(shift_set, 1)
            for k in range(2):
                link(dve.tensor_tensor(hp[k][:, :, :], hp[k][:, :, :], hrec[:, :, :], ALU.mult))
                dve.tensor_tensor(h0[k][:, :], hp[k][:, :, 0], chan[k][:, C_BMAT:C_BMAT + ORDER], ALU.add).then_inc(h0_ready, 1)
            for t in range(TH, TILES):
                patch_stats(t)
            variances(1)
            for hb in range(HB):
                t0 = hb * TH
                ts = slice(t0, t0 + TH)
                norm_scale(hb, 0)
                for t in range(t0, t0 + TH):
                    dve.wait_ge(emb_ready, t0 + min((t - t0) // 2 * 2 + 2, TH))
                    dve.scalar_tensor_tensor(out=u_tok[:, t, :], in0=ps_tok[:, t // TH, t % TH, 0:D], scalar=rstd[:, t:t + 1],
                                             in1=shift[:, :], op0=ALU.mult, op1=ALU.add).then_inc(emb_read, 1)
                dve.wait_ge(emb_read, t0 + TH)
                norm_stats(u_tok, hb)
            for hb in range(HB):
                t0 = hb * TH
                ts = slice(t0, t0 + TH)
                norm_scale(hb, 1)
                for t in range(t0, t0 + TH):
                    put(dve.tensor_scalar(h_tok[:, t, :], u_tok[:, t, :], mv[:, t, 0:1], rstd[:, t:t + 1], ALU.subtract, ALU.mult))
                settle()
                link(dve.tensor_tensor(h_tok[:, ts, :], h_tok[:, ts, :], rows_sb[:, 1:2, :].to_broadcast([P, TH, D]), ALU.mult))
                dve.wait_ge(pos_ready, 1)
                link(dve.tensor_tensor(h_tok[:, ts, :], h_tok[:, ts, :], pos_sb[:, :, :], ALU.add))
                link(dve.tensor_copy(h_tok[0:BH, t0, :], cls_sb[:, :]))
                norm_stats(h_tok, hb)
            for hb in range(HB):
                t0 = hb * TH
                ts = slice(t0, t0 + TH)
                norm_scale(hb, 2)
                for t in range(t0, t0 + TH):
                    dve.tensor_scalar(u_tok[:, t, :], h_tok[:, t, :], mv[:, t, 0:1], rstd[:, t:t + 1], ALU.subtract, ALU.mult).then_inc(utok_ready, 1)
            dve.wait_ge(utok_ready, TILES)
            for hb in range(HB):
                ts = slice(hb * TH, (hb + 1) * TH)
                put(dve.tensor_tensor(h_tok[:, ts, :], h_tok[:, ts, :], rows_sb[:, 3:4, :].to_broadcast([P, TH, D]), ALU.add))
            settle()

            def row_max(i):
                dve.wait_ge(xT_ready, i + 1)
                link(dve.tensor_reduce(mx[:, i, :].rearrange("p (h t) -> p h t", h=HB), ps_tok[:, :, 0:TH, 0:D], AX.X, ALU.max))
                dve.tensor_scalar(mx[:, i, :], mx[:, i, :], -1.0, None, ALU.mult).then_inc(nmx_ready, 1)

            def row_scale(i):
                dve.wait_ge(exp_done, TILES * (i + 1))
                dve.reciprocal(sums[:, i, :], sums[:, i, :]).then_inc(sum_recip_ready, 1)

            for n, (part, dst) in enumerate(((0, x[0]), (1, x[1]), (2, v))):
                dve.wait_ge(tap2_ready, 2 * n + 2)
                z = zs[n % 2]
                done = [0, 0]
                for back in (1, 2):
                    for m in range(2):
                        o = back * BH
                        tap = chan[m][:, C_TAP + 3 * part + 2 - back:C_TAP + 3 * part + 3 - back]
                        if back == 2:
                            dve.wait_ge(dve_c, done[m])
                        ins = dve.scalar_tensor_tensor(out=dst[m][:, :, o:], in0=z[m][:, :, 0:COLS - o], scalar=tap,
                                                       in1=dst[m][:, :, o:], op0=ALU.mult, op1=ALU.add)
                        if back == 1:
                            done[m] = put(ins)
                        else:
                            ins.then_inc(taps_done, 1)
                dve.wait_ge(taps_done, 2 * n + 2)
                if part == 1:
                    row_max(0)
                if part == 2:
                    for m in range(2):
                        dve.tensor_tensor(v[m][:, :, :], v[m][:, :, :], u[m][:, :, :], ALU.add).then_inc(v_base, 1)
            dve.wait_ge(v_base, 2)
            for i in range(ORDER):
                first = PE_LAGS[i]
                done = [put(dve.memset(y[m][:, :, 0:first * BH], 0.0)) for m in range(2)]
                for j in range(first, L):
                    o = j * BH
                    if i == 0 and j == first:
                        row_scale(0)
                        row_max(1)
                    if i == 0 and j == first + 6:
                        row_scale(1)
                    for m in range(2):
                        dve.wait_ge(dve_c, done[m])
                        if j == first:
                            ins = dve.tensor_scalar(y[m][:, :, o:REAL], v[m][:, :, 0:REAL - o], hp[m][:, i, j:j + 1], None, ALU.mult)
                        else:
                            ins = dve.scalar_tensor_tensor(out=y[m][:, :, o:REAL], in0=v[m][:, :, 0:REAL - o], scalar=hp[m][:, i, j:j + 1],
                                                           in1=y[m][:, :, o:REAL], op0=ALU.mult, op1=ALU.add)
                        done[m] = put(ins)
                dve.wait_ge(s_copied, 4 * (i + 1))
                settle()
                for n, (m, h) in enumerate(PARTS):
                    dve.wait_ge(conv_ready, len(PARTS) * i + n + 1)
                    here = y[m][:, h, 0:REAL].rearrange("p (b c) -> p b c", b=2)
                    bank = 4 * m + 2 * h
                    link(dve.tensor_tensor(here, here, ps[:, bank:bank + 2, 0:CB], ALU.add))
                    link(dve.tensor_tensor(y[m][:, h, 0:REAL], y[m][:, h, 0:REAL], soft[i][m][:, h, 0:REAL], ALU.mult))
                    dve.tensor_tensor(v[m][:, h, 0:REAL], v[m][:, h, 0:REAL], y[m][:, h, 0:REAL], ALU.add).then_inc(v_ready, 1)
                dve.wait_ge(v_ready, len(PARTS) * (i + 1))
            for hb in range(HB):
                t0 = hb * TH
                ts = slice(t0, t0 + TH)
                dve.wait_ge(o_ready, (hb + 1) * TH)
                link(dve.tensor_tensor(h_tok[:, ts, :], h_tok[:, ts, :], ps_tok[:, hb, 0:TH, 0:D], ALU.add))
                norm_stats(h_tok, hb)
            for hb in range(HB):
                t0 = hb * TH
                norm_scale(hb, 3)
                for t in range(t0, t0 + TH):
                    dve.tensor_scalar(u_tok[:, t, :], h_tok[:, t, :], mv[:, t, 0:1], rstd[:, t:t + 1], ALU.subtract, ALU.mult).then_inc(utok_ready, 1)
            for hb in range(HB):
                ts = slice(hb * TH, (hb + 1) * TH)
                dve.wait_ge(xhi_ready, 2 * (hb + 1))
                dve.tensor_tensor(xr[:, ts, 2 * P:3 * P], u_tok[:, ts, 0:P], xr[:, ts, 0:P], ALU.subtract).then_inc(xlo_ready, 1)
                for r in range(2):
                    ins = dve.tensor_tensor(xr[:, ts, 3 * P + r * DT:3 * P + (r + 1) * DT], u_tok[:, ts, P:D],
                                            xr[:, ts, P:P + DT], ALU.subtract)
                    if r:
                        ins.then_inc(xlo_ready, 1)
            dve.wait_ge(gate_ps, 1)
            G = gs
            link(dve.tensor_copy(G[:, 6, :].rearrange("p (h j e) -> p j h e", h=HB, j=TH),
                                 ps[:, 4, 0:TILES * E].rearrange("p (j h e) -> p j h e", j=TH, h=HB)))
            link(dve.tensor_scalar(G[:, 7, :], G[:, 6, :], -1.0, None, ALU.mult))
            dve.tensor_tensor(G[:, 0, :], G[:, 6, :], G[:, 7, :], ALU.max).then_inc(gate_abs, 1)
            dve.wait_ge(gate_exp, 1)
            dve.tensor_scalar(G[:, 2, :], G[:, 1, :], 1.0, None, ALU.add).then_inc(gate_exp1, 1)
            dve.wait_ge(gate_exp1, 1)
            link(dve.tensor_scalar(G[:, 8, :], G[:, 2, :], 1.0, None, ALU.subtract))
            link(dve.tensor_scalar(G[:, 9, :], G[:, 8, :], 0.0, None, ALU.is_equal))
            link(dve.tensor_tensor(G[:, 8, :], G[:, 8, :], G[:, 9, :], ALU.add))
            link(dve.reciprocal(G[:, 8, :], G[:, 8, :]))
            link(dve.tensor_tensor(G[:, 8, :], G[:, 8, :], G[:, 1, :], ALU.mult))
            dve.wait_ge(gate_log, 1)
            link(dve.tensor_tensor(G[:, 3, :], G[:, 3, :], G[:, 9, :], ALU.max))
            link(dve.tensor_tensor(G[:, 3, :], G[:, 3, :], G[:, 8, :], ALU.mult))
            dve.scalar_tensor_tensor(out=G[:, 4, :], in0=G[:, 6, :], scalar=0.0, in1=G[:, 3, :], op0=ALU.max, op1=ALU.add).then_inc(gate_softplus, 1)

            def v3(k):
                return G[:, k, :].rearrange("p (t e) -> p t e", e=E)

            def over(k):
                return gr[:, k, :].rearrange("p (t a) -> p t a", a=1).to_broadcast([P, TILES, E])

            def largest(k):
                if k == 0:
                    dve.wait_ge(gate_root, 1)
                    link(dve.tensor_tensor(v3(6), v3(5), gateb_sb[:, :].rearrange("p (a e) -> p a e", a=1).to_broadcast([P, TILES, E]), ALU.add))
                link(dve.tensor_reduce(gr[:, k, :], v3(6), AX.X, ALU.max))
                link(dve.tensor_tensor(v3(7), v3(6), over(k), ALU.is_equal))
                link(dve.tensor_tensor(G[:, 7, :], G[:, 7, :], tab[:, T_DOWN:T_DOWN + TILES * E], ALU.mult))
                link(dve.tensor_reduce(gr[:, 2, :], v3(7), AX.X, ALU.max))
                link(dve.tensor_tensor(v3(10 + k), v3(7), over(2), ALU.is_equal))
                if k == 0:
                    link(dve.scalar_tensor_tensor(out=G[:, 6, :], in0=G[:, 10, :], scalar=-1e30, in1=G[:, 6, :], op0=ALU.mult, op1=ALU.add))

            def chosen():
                real = tab[:, T_REAL:T_REAL + TILES].rearrange("p (t a) -> p t a", a=1).to_broadcast([P, TILES, E])
                for k in range(TOPK):
                    link(dve.tensor_tensor(v3(10 + k), v3(10 + k), real, ALU.mult))
                dve.tensor_tensor(G[:, 12, :], G[:, 10, :], G[:, 11, :], ALU.add).then_inc(chosen_ready, 1)

            def copy_counts():
                dve.wait_ge(counts_ready, 1)
                dve.tensor_copy(counts[:, :, :], ps[:, 7, 0:2 * TILES * E].rearrange("p (k n) -> p k n", k=2)).then_inc(counts_copied, 1)
                dve.wait_ge(counts_copied, 1)

            def sum_counts():
                link(dve.memset(run[:, 0, :], 0.0))
                for t in range(TILES):
                    link(dve.tensor_tensor(run[:, t + 1, :], run[:, t, :], counts[:, 1, t * E:(t + 1) * E], ALU.add))

            def first_tiles():
                sc = scratch[:, 0:E * TILES].rearrange("p (e k) -> p e k", e=E)
                link(dve.tensor_tensor(sc, run[:, TILES, :].rearrange("p (e a) -> p e a", a=1).to_broadcast([P, E, TILES]),
                                       tab[:, T_FULL:T_FULL + TILES].rearrange("p (a k) -> p a k", a=1).to_broadcast([P, E, TILES]), ALU.is_gt))
                link(dve.tensor_reduce(tiles_of[:, :], sc, AX.X, ALU.add))
                link(dve.memset(first_tile[:, 0:1], 0.0))
                for e in range(E):
                    link(dve.tensor_tensor(first_tile[:, e + 1:e + 2], first_tile[:, e:e + 1], tiles_of[:, e:e + 1], ALU.add))

            def token_slots():
                link(dve.tensor_tensor(G[:, 8, :], counts[:, 0, :], run[:, 0:TILES, :].rearrange("p t e -> p (t e)"), ALU.add))
                link(dve.tensor_scalar(gr[:, 0, 0:E], first_tile[:, 0:E], float(P), None, ALU.mult))
                link(dve.tensor_tensor(v3(8), v3(8), gr[:, 0, 0:E].rearrange("p (a e) -> p a e", a=1).to_broadcast([P, TILES, E]), ALU.add))
                for k in range(TOPK):
                    link(dve.tensor_tensor(G[:, 9, :], G[:, 8, :], G[:, 10 + k, :], ALU.mult))
                    link(dve.tensor_reduce(slot_f[:, k, :], v3(9), AX.X, ALU.add))
                dve.tensor_copy(slot_i[:, :, :], slot_f[:, :, :]).then_inc(slots_ready, 1)

            def tile_places():
                sc = scratch[0:1, :].rearrange("p (s e) -> p s e", s=ROUTED)
                link(dve.tensor_tensor(sc, tab[0:1, T_TILE:T_TILE + ROUTED].rearrange("p (s a) -> p s a", a=1).to_broadcast([1, ROUTED, E]),
                                       first_tile[0:1, 1:E + 1].rearrange("p (a e) -> p a e", a=1).to_broadcast([1, ROUTED, E]), ALU.is_ge))
                link(dve.tensor_reduce(place_f[:, :], sc, AX.X, ALU.add))
                link(dve.tensor_scalar(place_f[:, :], place_f[:, :], float(E - 1), 1.0, ALU.min, ALU.add))
                link(dve.tensor_scalar(place_f[:, :], place_f[:, :], float(SLOT), None, ALU.mult))
                dve.tensor_copy(place_i[:, :], place_f[:, :]).then_inc(place_ready, 1)

            def token_weights():
                for k in range(TOPK):
                    link(dve.tensor_tensor(G[:, 8, :], G[:, 10 + k, :], G[:, 5, :], ALU.mult))
                    link(dve.tensor_reduce(wk[:, k, :], v3(8), AX.X, ALU.add))
                link(dve.tensor_tensor(gr[:, 2, :], wk[:, 0, :], wk[:, 1, :], ALU.add))
                link(dve.tensor_scalar(gr[:, 2, :], gr[:, 2, :], 1e-6, None, ALU.max))
                link(dve.reciprocal(gr[:, 3, :], gr[:, 2, :]))
                for k in range(TOPK):
                    link(dve.tensor_tensor(wk[:, k, :], wk[:, k, :], gr[:, 3, :], ALU.mult))

            def clip(s, hh):
                dve.wait_ge(up_done, 2 * s + hh + 1)
                dve.tensor_scalar(uc[:, hh, :], ps[:, 2 + hh, 0:HI], LIMIT, -LIMIT, ALU.min, ALU.max).then_inc(clip_done, 1)

            def hidden(s, hh):
                k = 2 * s + hh
                dve.wait_ge(silu_done, k + 1)
                dve.wait_ge(clip_done, k + 1)
                at_least(dve, lo_done, k - 1)
                dve.scalar_tensor_tensor(out=hid[:, hh, :], in0=sg[:, hh, :], scalar=SILU_LIMIT, in1=uc[:, hh, :],
                                         op0=ALU.min, op1=ALU.mult).then_inc(h_ready, 1)

            def low(s, hh):
                k = 2 * s + hh
                dve.wait_ge(hi_done, k + 1)
                dve.tensor_tensor(hhl[:, hh, 1, :], hid[:, hh, :], hhl[:, hh, 0, :], ALU.subtract).then_inc(lo_done, 1)

            def copy_ha(s, par):
                dve.wait_ge(h_turned, 2 * s + 1)
                at_least(dve, down_done, s - 1)
                dve.tensor_copy(hT[:, par, 0, :], psum16(4, 2 * HI)).then_inc(ha_copied, 1)

            def add_y(s):
                dve.wait_ge(down_done, s + 1)
                dve.tensor_tensor(h_tok[:, s, :], h_tok[:, s, :], ps[:, 7, 0:D], ALU.add).then_inc(y_copied, 1)

            def copy_y(s, par, n_stored):
                dve.wait_ge(down_done, s + 1)
                at_least(dve, s_y[par], n_stored)
                dve.tensor_copy(ybuf[:, par, :], ps[:, 7, 0:D]).then_inc(y_copied, 1)

            def activate(s, hh):
                clip(s, hh)
                hidden(s, hh)
                low(s, hh)

            def router(s, hh):
                if (s, hh) == (0, 0):
                    largest(0)
                elif (s, hh) == (0, 1):
                    largest(1)
                    chosen()
                elif (s, hh) == (1, 0):
                    copy_counts()
                elif (s, hh) == (1, 1):
                    sum_counts()
                elif (s, hh) == (2, 0):
                    first_tiles()
                elif (s, hh) == (2, 1):
                    token_slots()
                elif (s, hh) == (3, 1):
                    tile_places()
                elif (s, hh) == (4, 1):
                    token_weights()

            for s in range(TILES):
                for hh in range(2):
                    activate(s, hh)
                    if hh == 1 and s > 0:
                        add_y(s - 1)
                    if hh == 1:
                        copy_ha(s, s % 2)
                    router(s, hh)

            def tiles(s0, n, stored=None):
                for i in range(n):
                    s, par = s0 + i, i % 2
                    activate(s, 0)
                    activate(s, 1)
                    if stored is None and i == 0:
                        add_y(s - 1)
                    else:
                        copy_y(s - 1, 1 - par, 16 * ((i - 1) // 2 + (0 if stored is None else stored)))
                    copy_ha(s, par)

            tiles(TILES, GROUP)
            with dve.Fori(1, GROUPS) as q:
                tiles(q * GROUP + TILES, GROUP, stored=q * (GROUP // 2))
            tiles(NT - 2, 2, stored=(ROUTED - 2) // 2)
            copy_y(NT - 1, 1, 16 * (ROUTED // 2 - 1))
            for t in range(TILES + 1):
                for k in range(TOPK):
                    a = t - k
                    if not 0 <= a < TILES:
                        continue
                    if k == 0:
                        dve.wait_ge(s_gather[a], 16)
                    else:
                        dve.wait_ge(first_added, a + 1)
                    n = min(LT, L - (a % TH) * LT) * BH
                    dve.scalar_tensor_tensor(out=h_tok[0:n, a, :], in0=gathered[0:n, a, k, :], scalar=wk[0:n, k, a:a + 1], in1=h_tok[0:n, a, :],
                                             op0=ALU.mult, op1=ALU.add).then_inc((first_added, summed)[k], 1)

        @block.tensor
        def _(pe):
            def mm(o, lhsT, rhs, first, last):
                return pe.matmul(o, lhsT, rhs, start=first, stop=last, skip_group_check=True)

            pe.wait_ge(s_small, NSMALL)
            pe.wait_ge(ones_set, 1)
            pe.wait_ge(wg_ready, 2 * FC)
            for c in range(FC):
                last = mm(ps[:, 5, 0:D], ones[:, :], wg_sb[:, c, :], c == 0, c == FC - 1)
            last.then_inc(cols_ready, 1)
            for c in range(FC):
                last = mm(ps[:, 4, 0:D], b1_wide[:, c, :], w_sb[:, c, :], c == 0, c == FC - 1)
            last.then_inc(shift_ps, 1)
            pe.wait_ge(habs_ready, 2)
            mm(ps[:, 4, 256:256 + ORDER * L], ones[:, :], habs[0][:, :, :].rearrange("p o l -> p (o l)"), True, False)
            mm(ps[:, 4, 256:256 + ORDER * L], ones[0:64, :], habs[1][0:64, :, :].rearrange("p o l -> p (o l)"), False, True).then_inc(hsum_ready, 1)

            def turn_patches(t):
                pe.wait_ge(s_x[t % KEPT], 16 * (t // KEPT + 1))
                for h in range(2):
                    at_least(pe, xf_copied, 2 * t + h - 1)
                    for i in range(FC // 2):
                        c = h * FC // 2 + i
                        last = pe.transpose(ps[:, 6 + h, i * P:(i + 1) * P], xt[:, t % KEPT, c * P:(c + 1) * P], id_sb[:, :])
                    last.then_inc(xf_turned, 1)

            def embed(t):
                pe.wait_ge(xf_copied, 2 * t + 2)
                for c in range(FC):
                    last = mm(ps_tok[:, t // TH, t % TH, 0:D], xf[:, t % TURNED, c, :], wg_sb[:, c, :], c == 0, c == FC - 1)
                last.then_inc(emb_ready, 1)

            turn_patches(0)
            pe.wait_ge(wc_ready, 1)
            for t in range(1, TILES):
                turn_patches(t)
                if t - 1 == TH:
                    pe.wait_ge(shift_set, 1)
                embed(t - 1)
            embed(TILES - 1)
            pe.wait_ge(emb_ready, TILES)

            def transpose_tail(hb, o, t, src=u_tok):
                if hb == 0:
                    return pe.transpose(ps_flat[0:DT, o:o + P], src[:, t, P:D], id_sb[:, :])
                return pe.transpose(ps_flat[:, o:o + P], src[:, t, D - P:D], id_sb[:, :])

            def transpose_u(n):
                for hb in range(HB):
                    for j in range(TH):
                        t = hb * TH + j
                        pe.wait_ge(utok_ready, n * TILES + t + 1)
                        o = hb * 2048 + j * P
                        pe.transpose(ps_flat[:, o:o + P], u_tok[:, t, 0:P], id_sb[:, :])
                        last = transpose_tail(hb, o + 1024, t)
                    last.then_inc(uT_ready, 1)

            pe.wait_ge(s_front, NFRONT)
            pe.wait_ge(emb_read, TILES)
            transpose_u(0)
            pe.wait_ge(u_ready, 4)
            k = 0

            def project(part):
                nonlocal k
                c0 = part * D
                for m in range(2):
                    for hb in range(HB if m == 0 else 1):
                        for s in range(2):
                            if k >= 3:
                                pe.wait_ge(z_copied, k - 2)
                            cs = slice(s * SPLIT, (s + 1) * SPLIT)
                            if m == 0:
                                o = ps[:, 5 + k % 3, 0:SPLIT]
                                mm(o, wlin[0][:, c0:c0 + P], u[0][:, hb, cs], True, False)
                                last = mm(o, wlin[1][half(hb), c0:c0 + P], u[1][half(hb), 0, cs], False, True)
                            else:
                                for h in range(HB):
                                    o = ps[half(h), 5 + k % 3, 0:SPLIT]
                                    mm(o, wlin[0][:, c0 + P:c0 + D], u[0][:, h, cs], True, False)
                                    last = mm(o, wlin[1][half(h), c0 + P:c0 + D], u[1][half(h), 0, cs], False, True)
                            last.then_inc(z_ready, 1)
                            k += 1

            def to_tokens(i):
                for t in range(TILES):
                    hb, j = divmod(t, TH)
                    cs = slice(j * P, (j + 1) * P)
                    pe.transpose(ps_tok[:, hb, j, 0:P], x[i][0][:, hb, cs], id_sb[:, :])
                    last = pe.transpose(ps_tok[:, hb, j, P:D], x[i][1][half(hb), 0, cs], id_sb[half(hb), half(hb)])
                last.then_inc(xT_ready, 1)

            def to_channels(i):
                pe.wait_ge(soft_ready, (i + 1) * TILES)
                for r in range(4):
                    at_least(pe, s_copied, 4 * i + r)
                    for j in range(TH):
                        t = (r % 2) * TH + j
                        o = 3072 + j * P
                        if r < 2:
                            last = pe.transpose(ps_flat[:, o:o + P], x_tok[i][:, t, 0:P], id_sb[:, :])
                        else:
                            last = transpose_tail(r - 2, o, t, x_tok[i])
                    last.then_inc(s_turned, 1)

            def long_conv(i):
                pe.wait_ge(diag_ready, 2 * sum(PE_LAGS[0:i + 1]))
                for n, (m, h) in enumerate(PARTS):
                    if i > 0:
                        pe.wait_ge(v_ready, len(PARTS) * (i - 1) + n + 1)
                    for j in range(PE_LAGS[i]):
                        for b in range(2):
                            lo, hi = max(j * BH, b * CB), (b + 1) * CB
                            last = mm(ps[:, 4 * m + 2 * h + b, lo - b * CB:CB], diag[i][:, m, j, :], v[m][:, h, lo - j * BH:hi - j * BH],
                                      j == 0, j == PE_LAGS[i] - 1)
                    last.then_inc(conv_ready, 1)

            project(0)
            project(1)
            project(2)
            pe.wait_ge(taps_done, 2)
            pe.wait_ge(z_copied, k)
            to_tokens(0)
            pe.wait_ge(taps_done, 4)
            pe.wait_ge(exp_done, TILES)
            to_tokens(1)
            to_channels(0)
            pe.wait_ge(exp_done, 2 * TILES)
            pe.wait_ge(v_base, 2)
            long_conv(0)
            to_channels(1)
            long_conv(1)
            pe.wait_ge(wout_ready, 3)
            for t in range(TILES):
                hb, j = divmod(t, TH)
                pe.wait_ge(v_ready, len(PARTS) * (ORDER - 1) + (2 if t < TH - 1 else 3))
                cs = slice(j * P, (j + 1) * P)
                mm(ps_tok[:, t // TH, t % TH, 0:D], v[0][:, hb, cs], wout[0][:, :], True, False)
                mm(ps_tok[:, t // TH, t % TH, 0:D], v[1][half(hb), 0, cs], wout[1][half(hb), :], False, True).then_inc(o_ready, 1)
            pe.wait_ge(var_ready, 8)
            transpose_u(1)
            pe.wait_ge(u_ready, 8)
            def count():
                pe.wait_ge(chosen_ready, 1)
                n8 = TILES * E
                mm(ps[:, 7, 0:n8], upper_sb[:, :], gs[:, 12, :], True, True)
                mm(ps[:, 7, n8:2 * n8], ones[:, :], gs[:, 12, :], True, True).then_inc(counts_ready, 1)

            def turn_x(s, rows):
                at_least(pe, x_copied, s)
                for a in range(4):
                    last = pe.transpose(psum16(6, ROW)[:, a * P:(a + 1) * P], rows[:, a * P:(a + 1) * P], id16[:, :])
                last.then_inc(x_turned, 1)

            def up(s, par, hh, place):
                pe.wait_ge(x_copied, s + 1)
                at_least(pe, h_ready, 2 * s + hh - 1)
                for n in range(2):
                    for i, (a, b) in enumerate(((0, 0), (0, 1), (2, 0), (1, 2), (3, 2))):
                        at = place + (n * 3 * I + b * I + hh * HI)
                        last = mm(ps[:, 2 * n + hh, 0:HI], xT[:, par, a, :], w16[:, bass.ds(at, HI)], i == 0, i == 4)
                last.then_inc(up_done, 1)

            def turn_h(s, hh):
                k = 2 * s + hh
                pe.wait_ge(lo_done, k + 1)
                at_least(pe, (ha_copied, hb_copied)[hh], s)
                for a in range(2 * IC // 2):
                    last = pe.transpose(psum16(4 + hh, 2 * HI)[:, a * P:(a + 1) * P],
                                        hhl[:, hh, :, :].rearrange("p a n -> p (a n)")[:, a * P:(a + 1) * P], id16[:, :])
                last.then_inc(h_turned, 1)

            def down(s, par, place):
                pe.wait_ge(ha_copied, s + 1)
                pe.wait_ge(hb_copied, s + 1)
                at_least(pe, y_copied, s)
                for c in range(IC):
                    hh, i = divmod(c, IC // 2)
                    for a, b in ((0, 0), (0, 1), (1, 0)):
                        at = place + (W2_AT + b * IC * D + c * D)
                        last = mm(ps[:, 7, 0:D], hT[:, par, hh, a * HI + i * P:a * HI + (i + 1) * P], w16[:, bass.ds(at, D)],
                                  c == 0 and a == b == 0, c == IC - 1 and a == 1)
                last.then_inc(down_done, 1)

            def place_of(s):
                return pe.value_load(place_i[0:1, bass.ds(s - TILES, 1)], min_val=0, max_val=E * SLOT)

            def turn_loaded(s, par, n):
                pe.wait_ge(s_xs[par], n)
                turn_x(s, xs[:, par, :])

            def turn_shared(s):
                pe.wait_ge(xlo_ready, 2 * (s // TH + 1))
                turn_x(s, xr[:, s, :])

            pe.wait_ge(id16_set, 1)
            turn_shared(0)
            for j in range(TH):
                cs = slice(j * P, (j + 1) * P)
                mm(ps[:, 4, HB * j * E:HB * (j + 1) * E], u[1][:, 0, cs], gate[1][:, :], True, False)
                for hb in range(HB):
                    last = mm(ps[:, 4, (HB * j + hb) * E:(HB * j + hb + 1) * E], u[0][:, hb, cs], gate[0][:, :], False, hb == HB - 1)
            last.then_inc(gate_ps, 1)
            pe.wait_ge(lo_split, CHUNKS)
            for s in range(TILES):
                up(s, s % 2, 0, 0)
                if s > 0:
                    turn_h(s - 1, 1)
                if s == 1:
                    count()
                up(s, s % 2, 1, 0)
                if s + 1 < TILES:
                    turn_shared(s + 1)
                else:
                    turn_loaded(s + 1, 0, 16)
                if s > 0:
                    if s == 1:
                        pe.wait_ge(counts_copied, 1)
                    down(s - 1, 1 - s % 2, 0)
                turn_h(s, 0)
            pe.wait_ge(place_ready, 1)
            pe.wait_ge(lo_split, NX * CHUNKS)

            def tiles(s0, n, loads, first=False, last=False):
                here = place_of(s0)
                before = 0 if first else place_of(s0 - 1)
                for i in range(n):
                    s, par = s0 + i, i % 2
                    up(s, par, 0, here)
                    turn_h(s - 1, 1)
                    up(s, par, 1, here)
                    if not (last and i == n - 1):
                        turn_loaded(s + 1, 1 - par, 16 * (loads + (i + 1) // 2))
                    down(s - 1, 1 - par, before)
                    before = here
                    if i + 1 < n:
                        here = place_of(s + 1)
                    turn_h(s, 0)

            tiles(TILES, GROUP, 1, first=True)
            with pe.Fori(1, GROUPS) as q:
                tiles(q * GROUP + TILES, GROUP, q * (GROUP // 2) + 1)
            tiles(NT - 2, 2, ROUTED // 2, last=True)
            turn_h(NT - 1, 1)
            down(NT - 1, 1, place_of(NT - 1))


def kernel(**inputs):
    import numpy as np
    import concourse.bacc as bacc
    from concourse.bass_utils import run_bass_kernel_spmd

    a = {k: np.ascontiguousarray(v) for k, v in inputs.items()}
    f32 = np.float32

    def tiles(m):
        n = m.shape[2]
        padded = np.zeros((HB, LP, BH, n), f32)
        padded[:, :m.shape[1]] = m.reshape(HB, BH, m.shape[1], n).transpose(0, 2, 1, 3)
        return padded.reshape(TILES, P, n)

    def wide(row):
        return np.ascontiguousarray(np.broadcast_to(row, (P,) + row.shape))

    def split(m):
        return np.ascontiguousarray(m[:P]), np.concatenate([m[P:], m[P:]])

    patches = a["x"].reshape(B, 3, 6, 16, 6, 16).transpose(0, 2, 4, 3, 5, 1).reshape(B, 36, PD)
    patches = np.concatenate([np.zeros((B, 1, PD), f32), patches], axis=1)
    xtok = tiles(patches)
    pos = np.zeros((LP, D), f32)
    pos[:L] = a["L0_tok_pos_embed"][0]
    chan = np.concatenate([a["L0_attn_b_lin"].reshape(3, D).T,
                           a["L0_attn_conv_w"].reshape(3, D, 3).transpose(1, 0, 2).reshape(D, 9),
                           a["L0_attn_conv_b"].reshape(3, D).T, a["L0_attn_alphas"].reshape(D, 1),
                           a["L0_attn_win_b"].reshape(D, 1), a["L0_attn_Bmat"].reshape(ORDER, D).T], axis=1)
    ins = {
        "xtok": xtok,
        "pos": pos.reshape(TH, LT, 1, D).repeat(BH, 2).reshape(TH, P, D).transpose(1, 0, 2),
        "ident": np.eye(P, dtype=f32),
        "steps": wide(np.linspace(0.0, 1.0, 512, dtype=f32)[:L]),
        "w_in": a["L0_tok_W"].reshape(FC, P, D).transpose(1, 0, 2),
        "g1": a["L0_tok_ln1_g"].reshape(FC, P).T,
        "b1": a["L0_tok_ln1_b"].reshape(FC, P).T,
        "rows": wide(np.stack([a["L0_tok_b"], a["L0_tok_ln2_g"], a["L0_tok_ln2_b"], a["L0_attn_b_out"]])),
        "cls": np.broadcast_to(a["L0_tok_cls_token"], (BH, D)),
    }
    ins["wlin_m"], ins["wlin_t"] = split(a["L0_attn_W_lin"].T)
    ins["chan_m"], ins["chan_t"] = split(chan)
    ins["hp_m"], ins["hp_t"] = split(a["L0_attn_h_param"].transpose(1, 0, 2)[:, :, :L])
    ins["wout_m"], ins["wout_t"] = split(a["L0_attn_W_out"].T)
    ins["gate_m"] = a["L0_ffn_gate_w"][:P]
    ins["gate_t"] = np.zeros((P, HB * E), f32)
    for hb in range(HB):
        ins["gate_t"][64 * hb:64 * hb + 64, hb * E:(hb + 1) * E] = a["L0_ffn_gate_w"][P:]
    ins["gate_b"] = wide(a["L0_ffn_gate_bias"])
    table = np.zeros((P, NTAB), f32)
    where = np.arange(P)[:, None] // BH + LT * (np.arange(TILES)[None, :] % TH)
    table[:, T_REAL:T_REAL + TILES] = where < L
    table[:, T_DOWN:T_FULL] = np.tile(np.arange(E, 0, -1), TILES)
    table[:, T_FULL:T_TILE] = P * np.arange(TILES)
    table[:, T_TILE:T_ID] = np.arange(ROUTED)
    table[:, T_ID:] = np.arange(P)[:, None] + P * np.concatenate([np.arange(TILES), TOPK * TILES + np.arange(ROUTED)])
    ins["tables"] = table
    ins["upper"] = np.triu(np.ones((P, P), f32), 1)
    for n in ("w1", "w3", "w2"):
        ins[n] = np.concatenate([a["L0_ffn_" + n + "s"][None], a["L0_ffn_" + n]])

    nc = bacc.Bacc("TRN2", target_bir_lowering=False, num_devices=1)
    arrays, args = {}, []
    for name, m in ins.items():
        arrays["in_" + name] = np.ascontiguousarray(m)
        args.append(nc.dram_tensor("in_" + name, m.shape, F32, kind="ExternalInput").ap())
    args.append(nc.dram_tensor("out_0", (B, L, D), F32, kind="ExternalOutput").ap())
    build(nc, *args)
    r = run_bass_kernel_spmd(nc, [arrays], core_ids=[0])
    return r.results[0]["out_0"]
```
